# Optimizing a Trainium2 kernel written in Bass

```python
import numpy as np
import jax
import jax.numpy as jnp

def _softmax(x, axis=-1):
    return jax.nn.softmax(x, axis=axis)

def _gelu(x):
    return jax.nn.gelu(x, approximate=True)

def _silu(x):
    return jax.nn.silu(x)

def _sigmoid(x):
    return jax.nn.sigmoid(x)

def _layernorm(x, axis=-1, eps=1e-05):
    m = jnp.mean(x, axis=axis, keepdims=True)
    v = jnp.var(x, axis=axis, keepdims=True)
    return (x - m) / jnp.sqrt(v + eps)

def _scatter_add(tgt, idx, src, axis=0):
    return tgt.at[idx].add(src)

def _segment_sum(src, seg, n):
    return jax.ops.segment_sum(src, seg, n)
kernel_name = 'mk_flamingo_gated_d1_seqx_r4_db2c49'

def setup_inputs(seed: int=0):
    np.random.seed(seed)
    _w = jnp.asarray

    def _rec_inputs():
        import jax
        import jax.numpy as jnp
        _rk = jax.random.key(seed)
        x = -0.0002928 + 1 * jax.random.normal(jax.random.fold_in(_rk, 1), (8, 256, 256), jnp.float32)
        _lenS = 256 - jax.random.randint(jax.random.fold_in(_rk, 7), (8,), 0, max(1, 256 // 4) + 1, jnp.int32)
        _lenS2 = 120 - jax.random.randint(jax.random.fold_in(_rk, 8), (8,), 0, max(1, 120 // 4) + 1, jnp.int32)
        _ctx_512P = jax.random.normal(jax.random.fold_in(_rk, 11), (8, 16, 128), jnp.float32)
        _ctx_512c = jax.random.dirichlet(jax.random.fold_in(_rk, 511), 0.3 * jnp.ones((16,), jnp.float32), (8, 120))
        _ctx_512t = jnp.einsum('bsk,bkd->bsd', _ctx_512c, _ctx_512P)
        _ctx_512t = _ctx_512t * jax.lax.rsqrt(jnp.mean(jnp.square(_ctx_512t)) + 1e-12) * 0.953939
        ctx_512 = -1.52775e-05 + 0.999936 * (_ctx_512t + 0.3 * jax.random.normal(jax.random.fold_in(_rk, 611), (8, 120, 128), jnp.float32))
        _g = jax.random.normal(jax.random.fold_in(_rk, 9001), (2, 1), jnp.float32)
        _g = jnp.sign(_g) * jnp.maximum(jnp.abs(_g), 1.0) + (_g == 0) * 1.0
        g_xattn = _g[0]
        g_ffn = _g[1]
        return (x, ctx_512, g_xattn, g_ffn)
    x, ctx_512, g_xattn, g_ffn = _rec_inputs()

    def _L0_xattn_setup():
        import jax, jax.numpy as jnp
        import numpy as np
        NUM_HEADS = 16
        HEAD_DIM = 64
        Q_DIM = 256
        KV_DIM = 128
        INNER = NUM_HEADS * HEAD_DIM
        key = jax.random.key(seed)
        ks = jax.random.split(key, 7)
        B, N, M = (32, 128, 512)
        q = jax.random.normal(ks[0], (B, N, Q_DIM), dtype=jnp.float32)
        kv = jax.random.normal(ks[1], (B, M, KV_DIM), dtype=jnp.float32)
        Wq = jax.random.normal(ks[2], (Q_DIM, INNER), dtype=jnp.float32) / np.sqrt(Q_DIM)
        Wk = jax.random.normal(ks[3], (KV_DIM, INNER), dtype=jnp.float32) / np.sqrt(KV_DIM)
        Wv = jax.random.normal(ks[4], (KV_DIM, INNER), dtype=jnp.float32) / np.sqrt(KV_DIM)
        Wo = jax.random.normal(ks[5], (INNER, Q_DIM), dtype=jnp.float32) / np.sqrt(INNER)
        bo = jax.random.normal(ks[6], (Q_DIM,), dtype=jnp.float32) * 0.01
        return {'q': q, 'kv': kv, 'Wq': Wq, 'Wk': Wk, 'Wv': Wv, 'Wo': Wo, 'bo': bo}
    _L0_xattn_all = _L0_xattn_setup()
    _L0_xattn_in = {k: v for k, v in _L0_xattn_all.items() if k in ('Wq', 'Wk', 'Wv', 'Wo', 'bo')}
    del _L0_xattn_all

    def _L0_ffn_setup():
        import jax, jax.numpy as jnp
        import numpy as np
        LN_EPS = 1e-05
        NORM_EPS = 1e-12

        def _layernorm(x, gamma, beta):
            mu = x.mean(axis=-1, keepdims=True)
            var = ((x - mu) ** 2).mean(axis=-1, keepdims=True)
            return (x - mu) * jax.lax.rsqrt(var + LN_EPS) * gamma + beta

        def _l2norm(x, axis):
            n = jnp.sqrt((x ** 2).sum(axis=axis, keepdims=True))
            return x / jnp.maximum(n, NORM_EPS)
        key = jax.random.key(seed)
        ks = jax.random.split(key, 4)
        B, N, D, E, S, H = (64, 64, 256, 16, 16, 64)
        x = jax.random.normal(ks[0], (B, N, D), dtype=jnp.float32)
        mu = jax.random.normal(ks[1], (D, E, S), dtype=jnp.float32) / np.sqrt(D)
        w1 = jax.random.normal(ks[2], (E, D, H), dtype=jnp.float32) * np.sqrt(2.0 / D)
        w2 = jax.random.normal(ks[3], (E, H, D), dtype=jnp.float32) * np.sqrt(2.0 / (H + D))
        return {'x': x, 'ln_gamma': jnp.ones((D,), jnp.float32), 'ln_beta': jnp.zeros((D,), jnp.float32), 'mu': mu, 'scale': jnp.ones((1,), jnp.float32), 'w1': w1, 'b1': jnp.zeros((E, H), jnp.float32), 'w2': w2, 'b2': jnp.zeros((E, D), jnp.float32)}
    _L0_ffn_all = _L0_ffn_setup()
    _L0_ffn_in = {k: v for k, v in _L0_ffn_all.items() if k in ('ln_gamma', 'ln_beta', 'mu', 'scale', 'w1', 'b1', 'w2', 'b2')}
    del _L0_ffn_all
    return {'x': x, 'ctx_512': ctx_512, 'g_xattn': g_xattn, 'g_ffn': g_ffn, 'L0_xattn_Wq': _L0_xattn_in['Wq'], 'L0_xattn_Wk': _L0_xattn_in['Wk'], 'L0_xattn_Wv': _L0_xattn_in['Wv'], 'L0_xattn_Wo': _L0_xattn_in['Wo'], 'L0_xattn_bo': _L0_xattn_in['bo'], 'L0_ffn_ln_gamma': _L0_ffn_in['ln_gamma'], 'L0_ffn_ln_beta': _L0_ffn_in['ln_beta'], 'L0_ffn_mu': _L0_ffn_in['mu'], 'L0_ffn_scale': _L0_ffn_in['scale'], 'L0_ffn_w1': _L0_ffn_in['w1'], 'L0_ffn_b1': _L0_ffn_in['b1'], 'L0_ffn_w2': _L0_ffn_in['w2'], 'L0_ffn_b2': _L0_ffn_in['b2']}

def reference(x, ctx_512, g_xattn, g_ffn, L0_xattn_Wq, L0_xattn_Wk, L0_xattn_Wv, L0_xattn_Wo, L0_xattn_bo, L0_ffn_ln_gamma, L0_ffn_ln_beta, L0_ffn_mu, L0_ffn_scale, L0_ffn_w1, L0_ffn_b1, L0_ffn_w2, L0_ffn_b2):
    import jax
    import jax.numpy as jnp

    def _L0_xattn_ref(q, kv, Wq, Wk, Wv, Wo, bo):
        import jax, jax.numpy as jnp
        import numpy as np
        NUM_HEADS = 16
        HEAD_DIM = 64
        Q_DIM = 256
        KV_DIM = 128
        INNER = NUM_HEADS * HEAD_DIM
        B, N, _ = q.shape
        M = kv.shape[1]
        scale = HEAD_DIM ** (-0.5)
        qh = (q @ Wq).reshape(B, N, NUM_HEADS, HEAD_DIM).transpose(0, 2, 1, 3)
        kh = (kv @ Wk).reshape(B, M, NUM_HEADS, HEAD_DIM).transpose(0, 2, 1, 3)
        vh = (kv @ Wv).reshape(B, M, NUM_HEADS, HEAD_DIM).transpose(0, 2, 1, 3)
        scores = jnp.einsum('bhnd,bhmd->bhnm', qh, kh) * scale
        attn = jax.nn.softmax(scores, axis=-1)
        out = jnp.einsum('bhnm,bhmd->bhnd', attn, vh)
        out = out.transpose(0, 2, 1, 3).reshape(B, N, INNER)
        return out @ Wo + bo

    def _L0_ffn_ref(x, ln_gamma, ln_beta, mu, scale, w1, b1, w2, b2):
        import jax, jax.numpy as jnp
        import numpy as np
        LN_EPS = 1e-05
        NORM_EPS = 1e-12

        def _layernorm(x, gamma, beta):
            mu = x.mean(axis=-1, keepdims=True)
            var = ((x - mu) ** 2).mean(axis=-1, keepdims=True)
            return (x - mu) * jax.lax.rsqrt(var + LN_EPS) * gamma + beta

        def _l2norm(x, axis):
            n = jnp.sqrt((x ** 2).sum(axis=axis, keepdims=True))
            return x / jnp.maximum(n, NORM_EPS)
        B, N, D = x.shape
        _, E, S = mu.shape
        xn = _layernorm(x, ln_gamma, ln_beta)
        x_unit = _l2norm(xn, axis=-1)
        mu_unit = _l2norm(mu, axis=0)
        logits = jnp.einsum('bnd,des->bnes', x_unit * scale, mu_unit)
        dispatch = jax.nn.softmax(logits, axis=1)
        combine = jax.nn.softmax(logits.reshape(B, N, E * S), axis=-1).reshape(B, N, E, S)
        slot_in = jnp.einsum('bnd,bnes->besd', xn, dispatch)
        h = jax.nn.gelu(jnp.einsum('besd,edh->besh', slot_in, w1) + b1[None, :, None, :], approximate=False)
        slot_out = jnp.einsum('besh,ehd->besd', h, w2) + b2[None, :, None, :]
        out = jnp.einsum('besd,bnes->bnd', slot_out, combine)
        return out
    x = x + jnp.tanh(g_xattn[0]) * _L0_xattn_ref(_layernorm(x, axis=-1), ctx_512, L0_xattn_Wq, L0_xattn_Wk, L0_xattn_Wv, L0_xattn_Wo, L0_xattn_bo)
    x = x + jnp.tanh(g_ffn[0]) * _L0_ffn_ref(_layernorm(x, axis=-1), L0_ffn_ln_gamma, L0_ffn_ln_beta, L0_ffn_mu, L0_ffn_scale, L0_ffn_w1, L0_ffn_b1, L0_ffn_w2, L0_ffn_b2)
    return x

_drawn_inputs = setup_inputs


def setup_inputs(seed=0):
    import zlib

    import numpy as np

    out = dict(_drawn_inputs(seed))
    spreads = {'L0_ffn_ln_gamma': (1.0, 0.6),
     'L0_ffn_ln_beta': (0.0, 0.715),
     'L0_ffn_b1': (0.0, 0.8),
     'L0_ffn_b2': (0.0, 0.366)}
    factors = {'L0_xattn_bo': 7.723, 'L0_ffn_mu': 8.0}
    for name, (base, spread) in spreads.items():
        noise = np.random.default_rng([zlib.crc32(name.encode()), seed]).standard_normal(out[name].shape)
        drawn = base * np.exp(spread * noise) if base else spread * noise
        out[name] = jnp.asarray(drawn.astype(out[name].dtype))
    for name, factor in factors.items():
        out[name] = (out[name] * factor).astype(out[name].dtype)
    return out
```

```python
from contextlib import ExitStack

import numpy as np
import concourse.bass as bass
from concourse import mybir

F32 = mybir.dt.float32
F32R = mybir.dt.float32r
ALU = mybir.AluOpType
ACT = mybir.ActivationFunctionType
AX = mybir.AxisListType

P = 128
HEAD = 64
LN_EPS = 1e-5
NORM_EPS = 1e-12
LN_SHIFT = 20



def rows(ap, p):
    return ap.rearrange("(t p) d -> p t d", p=p)


def flamingo_layer(nc, x, ctx_kv, g_xattn, g_ffn, Wq, Wk, Wv, Wo, bo, ln_gamma, ln_beta, mu, scale,
                   w1, b1, w2, b2, out):
    B, N, D = x.shape
    M, KV = ctx_kv.shape[1:]
    INNER = Wq.shape[1]
    PAIRS = INNER // P
    NT = N // P
    DC = D // P
    _, E, S = mu.shape
    ES = E * S
    EC = ES // P
    H = w1.shape[2]
    assert KV == P and D == 2 * P and N == 2 * P and ES == 2 * P and PAIRS % 4 == 0 and 4 * M <= 512
    K2 = 2 * M
    QK_SCALE = float(HEAD) ** -0.5
    EQ = 4
    SLOTS = S * B
    VR = 4
    SR = 4

    slot_out_dram = nc.dram_tensor("slot_out", (E, S, B, D), F32, kind="Internal").ap()

    with ExitStack() as top:
        def sb(stack, name, shape, dt=F32):
            return stack.enter_context(nc.sbuf_tensor(name, shape, dt))

        def sem(name):
            return top.enter_context(nc.semaphore(name))

        def bank(name):
            return top.enter_context(nc.psum_tensor(name, [P, 512], F32))

        scores_ps = [bank(f"scores_ps{i}") for i in range(2)]
        probT_ps = [bank(f"probT_ps{i}") for i in range(2)]
        proj_ps = bank("proj_ps")
        attn_ps = bank("attn_ps")
        misc_a = bank("misc_a")
        misc_b = bank("misc_b")

        x_all = sb(top, "x_all", [P, B, NT, D])
        wo_h = sb(top, "wo_h", [P, PAIRS, D], F32R)
        wo_l = sb(top, "wo_l", [P, PAIRS, D], F32R)
        mu_h = sb(top, "mu_h", [P, DC, ES], F32R)
        mu_l = sb(top, "mu_l", [P, DC, ES], F32R)
        combT_h = sb(top, "combT_h", [P, B, EC, N], F32R)
        combT_l = sb(top, "combT_l", [P, B, EC, N], F32R)
        slot_in = sb(top, "slot_in", [P, DC, E, S, B])
        attn_h = sb(top, "attn_h", [P, PAIRS, N], F32R)
        attn_l = sb(top, "attn_l", [P, PAIRS, N], F32R)
        xn2 = sb(top, "xn2", [P, NT, D])
        xn2_h = sb(top, "xn2_h", [P, NT, D], F32R)
        xn2_l = sb(top, "xn2_l", [P, NT, D], F32R)
        xn2T_h = sb(top, "xn2T_h", [P, DC, N], F32R)
        xn2T_l = sb(top, "xn2T_l", [P, DC, N], F32R)
        logit = sb(top, "logit", [P, NT, ES])
        dispT = sb(top, "dispT", [P, EC, N])
        disp_h = sb(top, "disp_h", [P, NT, ES], F32R)
        disp_l = sb(top, "disp_l", [P, NT, ES], F32R)
        comb = sb(top, "comb", [P, NT, ES])
        squares = sb(top, "squares", [P, NT, D])
        gamma = sb(top, "gamma", [P, D])
        beta = sb(top, "beta", [P, D])
        bo_t = sb(top, "bo_t", [P, D])
        ident = sb(top, "ident", [P, P])
        b1_in = sb(top, "b1_in", [E, H])
        b1T = sb(top, "b1T", [H, E])
        gates = sb(top, "gates", [P, 2])
        tanhs = sb(top, "tanhs", [P, 2])
        scale_t = sb(top, "scale_t", [P, 1])
        pause = sb(top, "pause", [P, 1])
        stats1 = sb(top, "stats1", [P, NT, 6])
        mv1 = sb(top, "mv1", [P, NT, 2])
        nt1 = sb(top, "nt1", [P, 5, NT])
        stats2 = sb(top, "stats2", [P, NT, 6])
        mv2 = sb(top, "mv2", [P, NT, 2])
        nt2 = sb(top, "nt2", [P, 5, NT])
        nt3 = sb(top, "nt3", [P, 7, NT])
        neg_max_slot = sb(top, "neg_max_slot", [P, EC])
        neg_max_all = sb(top, "neg_max_all", [P, NT])
        disp_sum = sb(top, "disp_sum", [P, EC])
        disp_rec = sb(top, "disp_rec", [P, EC])
        comb_sum = sb(top, "comb_sum", [P, NT])
        comb_rec = sb(top, "comb_rec", [P, NT])
        wq_raw = slot_in[:, :, :, :, :].rearrange("p c e s b -> p (c e s b)")[:, 0:DC * INNER]\
            .rearrange("p (c n) -> p c n", c=DC)
        wo_raw = slot_in[:, :, :, :, :].rearrange("p c e s b -> p (c e s b)")[:, DC * INNER:DC * INNER + PAIRS * D]\
            .rearrange("p (c n) -> p c n", c=PAIRS)

        with ExitStack() as attention:
            wq_h = sb(attention, "wq_h", [P, DC, INNER], F32R)
            wq_l = sb(attention, "wq_l", [P, DC, INNER], F32R)
            wk = sb(attention, "wk", [P, INNER])
            wv = sb(attention, "wv", [P, INNER])
            ctx_in = sb(attention, "ctx_in", [M, KV])
            ctxT = sb(attention, "ctxT", [P, M])
            ctxT_next = sb(attention, "ctxT_next", [P, M])
            xn = sb(attention, "xn", [P, NT, D])
            xT_h = sb(attention, "xT_h", [P, DC, N], F32R)
            xT_l = sb(attention, "xT_l", [P, DC, N], F32R)
            q_h = sb(attention, "q_h", [P, 2, N], F32R)
            q_l = sb(attention, "q_l", [P, 2, N], F32R)
            k_h = sb(attention, "k_h", [P, 2, K2], F32R)
            k_l = sb(attention, "k_l", [P, 2, K2], F32R)
            v_h = sb(attention, "v_h", [M, VR, 2, P], F32R)
            v_l = sb(attention, "v_l", [M, VR, 2, P], F32R)
            prob = sb(attention, "prob", [P, 2, NT, 2, M])
            probT_h = sb(attention, "probT_h", [M, 2, 2 * N], F32R)
            probT_l = sb(attention, "probT_l", [M, 2, 2 * N], F32R)
            neg_max = sb(attention, "neg_max", [P, 2, NT * 2])
            prob_sum = sb(attention, "prob_sum", [P, 2, NT * 2])
            prob_rec = sb(attention, "prob_rec", [P, 2, NT * 2])
            mu_raw = sb(attention, "mu_raw", [P, DC, ES])
            mu_sq = sb(attention, "mu_sq", [P, DC, ES])
            mu_nt = sb(attention, "mu_nt", [P, 5, ES])
            ones = sb(attention, "ones", [P, P])

        with ExitStack() as experts:
            w1_t = sb(experts, "w1_t", [P, E, DC, H])
            w2_t = sb(experts, "w2_t", [H + 1, E, D])
            hidT = sb(experts, "hidT", [H + 1, E, SLOTS])
            so_tx = sb(experts, "so_tx", [P, SR, 2, D])
            so_rx = sb(experts, "so_rx", [P, SR, EC, D])
            so_h = sb(experts, "so_h", [P, 2, EC, D], F32R)
            so_l = sb(experts, "so_l", [P, 2, EC, D], F32R)
            out_t = sb(experts, "out_t", [P, 2, NT, D])

        x0_loaded, x_loaded, ctx_loaded = sem("x0_loaded"), sem("x_loaded"), sem("ctx_loaded")
        wq_loaded, wkv_loaded, wo_loaded = sem("wq_loaded"), sem("wkv_loaded"), sem("wo_loaded")
        small_loaded, mu_loaded, exp_loaded = sem("small_loaded"), sem("mu_loaded"), sem("exp_loaded")
        consts, zeros_ready, ident_ready, tanh_ready, bo_ready = sem("consts"), sem("zeros_ready"), sem("ident_ready"), sem("tanh_ready"), sem("bo_ready")
        wqh_ready, wql_ready = sem("wqh_ready"), sem("wql_ready")
        woh_ready, wol_ready = sem("woh_ready"), sem("wol_ready")
        musq_ready, munorm_done, muss_ready = sem("musq_ready"), sem("munorm_done"), sem("muss_ready")
        muguess_ready, murn_ready, muunit_ready = sem("muguess_ready"), sem("murn_ready"), sem("muunit_ready")
        b1T_done, b1T_ready = sem("b1T_done"), sem("b1T_ready")
        muh_ready, mul_ready, mu_chain, mu_act = sem("muh_ready"), sem("mul_ready"), sem("mu_chain"), sem("mu_act")
        var1_ready, guess1_ready, xn_ready = sem("var1_ready"), sem("guess1_ready"), sem("xn_ready")
        xT_done, xTh_ready, xTl_ready = sem("xT_done"), sem("xTh_ready"), sem("xTl_ready")
        ctxT_done, ctxT_staged, ctxT_ready = sem("ctxT_done"), sem("ctxT_staged"), sem("ctxT_ready")
        norm1_chain, act_chain1 = sem("norm1_chain"), sem("act_chain1")
        proj_done, projh_ready, projl_ready = sem("proj_done"), sem("projh_ready"), sem("projl_ready")
        scores_done, negmax_ready, exp_done = sem("scores_done"), sem("negmax_ready"), sem("exp_done")
        rec_ready, prob_ready, probT_done = sem("rec_ready"), sem("prob_ready"), sem("probT_done")
        pth_ready, ptl_ready = sem("pth_ready"), sem("ptl_ready")
        attn_done, attnh_ready, attnl_ready = sem("attn_done"), sem("attnh_ready"), sem("attnl_ready")
        xb_ready, y_done, x1_ready = sem("xb_ready"), sem("y_done"), sem("x1_ready")
        var2_ready, guess2_ready, xn2_ready = sem("var2_ready"), sem("guess2_ready"), sem("xn2_ready")
        ss_ready, ssm_ready, guess3_ready, rs_ready = sem("ss_ready"), sem("ssm_ready"), sem("guess3_ready"), sem("rs_ready")
        xn2h_ready, xn2l_ready = sem("xn2h_ready"), sem("xn2l_ready")
        xn2T_done, xn2Th_ready, xn2Tl_ready = sem("xn2T_done"), sem("xn2Th_ready"), sem("xn2Tl_ready")
        logits_done, logit_ready = sem("logits_done"), sem("logit_ready")
        logitT_done, slotmax_ready, allmax_ready = sem("logitT_done"), sem("slotmax_ready"), sem("allmax_ready")
        dexp_ready, cexp_ready, dispT_ready, disp_done = sem("dexp_ready"), sem("cexp_ready"), sem("dispT_ready"), sem("disp_done")
        disph_ready, displ_ready = sem("disph_ready"), sem("displ_ready")
        comb_ready, combT_done, combTh_ready, combTl_ready = (
            sem("comb_ready"), sem("combT_done"), sem("combTh_ready"), sem("combTl_ready"))
        slotin_done, slotin_ready = sem("slotin_done"), sem("slotin_ready")
        ffn_chain, act_chain2, act_chain3 = sem("ffn_chain"), sem("act_chain2"), sem("act_chain3")
        ones_ready, hid_done, hid_ready = sem("ones_ready"), sem("hid_done"), sem("hid_ready")
        so_done, so_ready = sem("so_done"), sem("so_ready")
        so_sent = [sem(f"so_sent{i}") for i in range(SR)]
        so_back = [sem(f"so_back{i}") for i in range(SR)]
        soh_ready, sol_ready, mix_done, out_ready = sem("soh_ready"), sem("sol_ready"), sem("mix_done"), sem("out_ready")
        out_sent = [sem(f"out_sent{i}") for i in range(2)]

        def wait(eng, s, n):
            if isinstance(n, int) and n <= 0:
                return
            eng.wait_ge(s, n)

        def v_cols(v, p):
            blocks = v[:, p % VR, :, :].rearrange("m h (k d) -> m (h k) d", d=HEAD)
            return blocks[:, 0:4:3, :]

        def batches(eng, nc_eng, body):
            body(0, True, False)
            with nc_eng.Fori(1, B - 1) as b:
                body(b, False, False)
            body(B - 1, False, True)

        block = top.enter_context(nc.Block())

        @block.sync
        def _(sp):
            sp.dma_start(x_all[:, 0, :, :], rows(x[0, :, :], P)).then_inc(x0_loaded, 16)
            sp.dma_start(ctx_in[:, :], ctx_kv[0, :, :]).then_inc(ctx_loaded, 16)
            sp.dma_start(wk[:, :], Wk).then_inc(wkv_loaded, 16)
            sp.dma_start(wv[:, :], Wv).then_inc(wkv_loaded, 16)
            sp.dma_start(x_all[:, 1:B, :, :], x[1:B, :, :].rearrange("b (t p) d -> p b t d", p=P)).then_inc(x_loaded, 16)
            sp.dma_start(wo_raw, rows(Wo, P)).then_inc(wo_loaded, 16)
            sp.dma_start(mu_raw[:, :, :], mu.rearrange("(c p) e s -> p c (e s)", p=P)).then_inc(mu_loaded, 16)
            with nc.sync.Fori(1, B) as b:
                sp.wait_ge(ctxT_done, b)
                sp.dma_start(ctx_in[:, :], ctx_kv[bass.ds(b, 1), :, :].rearrange("o m k -> (o m) k")).then_inc(ctx_loaded, 16)
            sp.wait_ge(attn_done, B * PAIRS)
            sp.wait_ge(mul_ready, 1)
            sp.dma_start(w1_t[:, :, :, :], w1.rearrange("e (c p) h -> p e c h", p=P)).then_inc(exp_loaded, 16)
            sp.dma_start(w2_t[0:H, :, :], w2.rearrange("e h d -> h e d")).then_inc(exp_loaded, 16)
            sp.dma_start(w2_t[H:H + 1, :, :], b2.rearrange("(o e) d -> o e d", o=1)).then_inc(exp_loaded, 16)
            for j in range(E // 2):
                sp.wait_ge(so_ready, j + 1)
                sp.dma_start(slot_out_dram[2 * j:2 * j + 2, :, :, :].rearrange("e s b d -> (s b) e d"),
                             so_tx[:, j % SR, :, :]).then_inc(so_sent[j % SR], 16)
            for s in so_sent:
                sp.wait_ge(s, 16 * (E // 2 // SR))
            for b in range(B):
                if b >= SR:
                    sp.wait_ge(soh_ready, b - SR + 1)
                    sp.wait_ge(sol_ready, b - SR + 1)
                sp.dma_start(so_rx[:, b % SR, :, :],
                             slot_out_dram[:, :, b, :].rearrange("(c e) s d -> (e s) c d", c=EC)).then_inc(so_back[b % SR], 16)
            for s in out_sent:
                s_last = 16 * (B // 2)
                sp.wait_ge(s, s_last)

        @block.gpsimd
        def _(pool):
            pool.dma_start(gates[:, 0:1], g_xattn.partition_broadcast(P)).then_inc(small_loaded, 16)
            pool.dma_start(gates[:, 1:2], g_ffn.partition_broadcast(P)).then_inc(small_loaded, 16)
            pool.dma_start(scale_t[:, :], scale.partition_broadcast(P)).then_inc(small_loaded, 16)
            pool.dma_start(bo_t[:, :], bo.partition_broadcast(P)).then_inc(small_loaded, 16)
            pool.dma_start(gamma[:, :], ln_gamma.partition_broadcast(P)).then_inc(small_loaded, 16)
            pool.dma_start(beta[:, :], ln_beta.partition_broadcast(P)).then_inc(small_loaded, 16)
            pool.dma_start(b1_in[:, :], b1).then_inc(small_loaded, 16)
            nc.gpsimd.memset(ident[:, :], 0.0).then_inc(consts, 1)
            nc.gpsimd.memset(ones[:, :], 1.0).then_inc(consts, 1)
            pool.wait_ge(consts, 2)
            pool.affine_select(out=ident[:, :], in_=ident[:, :], compare_op=ALU.not_equal, fill=1.0,
                               base=0, pattern=[[-1, P]], channel_multiplier=1).then_inc(ident_ready, 1)

            def normalise(b, p):
                g = 8 * b + p
                r = p % 2
                pool.wait_ge(exp_done, g + 1)
                pool.wait_ge(rec_ready, g + 1)
                pr = prob[:, r, :, :, :].rearrange("p t h m -> p (t h) m")
                nc.gpsimd.tensor_tensor(pr, pr, prob_rec[:, r, :].unsqueeze(2).broadcast_to([P, NT * 2, M]),
                                        ALU.mult).then_inc(prob_ready, 1)

            def residual_bias(b):
                pool.wait_ge(xn_ready, b + 1)
                pool.wait_ge(bo_ready, 1)
                xb = x_all[:, bass.ds(b, 1), :, :].rearrange("p o t d -> p (o t) d")
                nc.gpsimd.tensor_tensor(xb, xb, bo_t[:, :].unsqueeze(1).broadcast_to([P, NT, D]),
                                        ALU.add).then_inc(xb_ready, 1)

            def first_prep(p):
                if p == 0:
                    pool.wait_ge(mu_loaded, 16)
                    nc.gpsimd.tensor_tensor(mu_sq[:, :, :], mu_raw[:, :, :], mu_raw[:, :, :], ALU.mult).then_inc(musq_ready, 1)
                if p < 4:
                    pool.wait_ge(woh_ready, p + 1)
                    c = slice(p * PAIRS // 4, (p + 1) * PAIRS // 4)
                    nc.gpsimd.tensor_tensor(wo_l[:, c, :], wo_raw[:, c, :], wo_h[:, c, :].bitcast(F32),
                                            ALU.subtract).then_inc(wol_ready, 1)
                if p == 5:
                    pool.wait_ge(murn_ready, 1)
                    nc.gpsimd.tensor_tensor(mu_sq[:, :, :], mu_raw[:, :, :],
                                            mu_nt[:, 4, :].unsqueeze(1).broadcast_to([P, DC, ES]),
                                            ALU.mult).then_inc(muunit_ready, 1)

            normalise(0, 0)

            def step_loop(b, first, last):
                for p in range(PAIRS):
                    if not (last and p == PAIRS - 1):
                        normalise(b, p + 1)
                    if first:
                        first_prep(p)
                    elif p == 0:
                        residual_bias(b - 1)

            batches(pool, nc.gpsimd, step_loop)
            residual_bias(B - 1)

        @block.scalar
        def _(act):
            for c in range(2):
                n = slice(c * INNER // 2, (c + 1) * INNER // 2)
                act.dma_start(wq_raw[:, :, n], rows(Wq, P)[:, :, n]).then_inc(wq_loaded, 16)

            def copy(dst, src, scale=1.0):
                return nc.scalar.activation(dst, src, ACT.Copy, scale=scale)

            def guess(dst, ln, a, chain, n, shift=0):
                nc.scalar.activation(ln, a, ACT.Ln, scale=float(2 ** shift)).then_inc(chain, 1)
                act.wait_ge(chain, n)
                return nc.scalar.activation(dst, ln, ACT.Exp, scale=-0.5)

            def guess1(b):
                act.wait_ge(var1_ready, b + 1)
                guess(nt1[:, 2, :], nt1[:, 1, :], nt1[:, 0, :], act_chain1, b + 1).then_inc(guess1_ready, 1)

            def xT_high(b):
                act.wait_ge(xT_done, b + 1)
                copy(xT_h[:, :, :].rearrange("p c n -> p (c n)"), misc_a[:, :]).then_inc(xTh_ready, 1)

            def ctxT_copy(b):
                act.wait_ge(ctxT_done, b + 1)
                wait(act, ctxT_ready, b)
                copy(ctxT_next[:, :], misc_a[:, 0:M]).then_inc(ctxT_staged, 1)

            def ctxT_move(b):
                act.wait_ge(ctxT_staged, b + 1)
                wait(act, proj_done, 8 * b)
                copy(ctxT[:, :], ctxT_next[:, :]).then_inc(ctxT_ready, 1)

            def proj_high(b, p):
                g, r = 8 * b + p, p % 2
                act.wait_ge(proj_done, g + 1)
                wait(act, scores_done, g - 1)
                wait(act, attn_done, g - VR + 1)
                copy(q_h[:, r, :], proj_ps[:, 0:N], QK_SCALE)
                for h in range(2):
                    c = slice(h * HEAD, (h + 1) * HEAD)
                    copy(k_h[c, r, h * M:(h + 1) * M], proj_ps[c, N:N + M])
                copy(v_cols(v_h, p), proj_ps[0:M, N + M:N + M + P].rearrange("m (h d) -> m h d", h=2)).then_inc(projh_ready, 1)

            def exps(b, p):
                g, r = 8 * b + p, p % 2
                act.wait_ge(negmax_ready, g + 1)
                wait(act, probT_done, g - 1)
                wait(act, rec_ready, g - 1)
                for t in range(NT):
                    for h in range(2):
                        j = 2 * t + h
                        last = nc.scalar.activation(prob[:, r, t, h, :], scores_ps[r][:, j * M:(j + 1) * M], ACT.Exp,
                                                    bias=neg_max[:, r, j:j + 1], accum_out=prob_sum[:, r, j:j + 1])
                last.then_inc(exp_done, 1)

            def probT_high(b, p):
                g, r = 8 * b + p, p % 2
                act.wait_ge(probT_done, g + 1)
                wait(act, attn_done, g - 1)
                copy(probT_h[:, r, :], probT_ps[r][0:M, :]).then_inc(pth_ready, 1)

            def attn_high(b, p):
                g = 8 * b + p
                act.wait_ge(attn_done, g + 1)
                if p == 0:
                    wait(act, y_done, b)
                copy(attn_h[:, p, :], attn_ps[:, 0:N]).then_inc(attnh_ready, 1)

            def guess2(b):
                act.wait_ge(var2_ready, b + 1)
                guess(nt2[:, 2, :], nt2[:, 1, :], nt2[:, 0, :], act_chain2, b + 1).then_inc(guess2_ready, 1)

            def square_sums(b):
                act.wait_ge(xn2_ready, b + 1)
                wait(act, ssm_ready, b)
                for t in range(NT):
                    last = nc.scalar.activation(squares[:, t, :], xn2[:, t, :], ACT.Square, accum_out=nt3[:, 5, t:t + 1])
                last.then_inc(ss_ready, 1)
                wait(act, slotin_done, b)
                copy(xn2_h[:, :, :], xn2[:, :, :]).then_inc(xn2h_ready, 1)

            def guess3(b):
                act.wait_ge(ssm_ready, b + 1)
                guess(nt3[:, 2, :], nt3[:, 1, :], nt3[:, 0, :], act_chain3, b + 1, LN_SHIFT).then_inc(guess3_ready, 1)

            def xn2T_high(b):
                act.wait_ge(xn2T_done, b + 1)
                copy(xn2T_h[:, :, :].rearrange("p c n -> p (c n)"), misc_b[:, :]).then_inc(xn2Th_ready, 1)

            def logits_scaled(b):
                act.wait_ge(logits_done, b + 1)
                act.wait_ge(rs_ready, b + 1)
                wait(act, cexp_ready, b)
                for t in range(NT):
                    last = copy(logit[:, t, :], misc_a[:, t * ES:(t + 1) * ES], nt3[:, 6, t:t + 1])
                last.then_inc(logit_ready, 1)

            def comb_exp(b):
                act.wait_ge(allmax_ready, b + 1)
                wait(act, combT_done, b)
                for t in range(NT):
                    last = nc.scalar.activation(comb[:, t, :], logit[:, t, :], ACT.Exp, bias=neg_max_all[:, t:t + 1],
                                                accum_out=comb_sum[:, t:t + 1])
                last.then_inc(cexp_ready, 1)

            def disp_exp(b):
                act.wait_ge(slotmax_ready, b + 1)
                wait(act, disp_done, b)
                for c in range(EC):
                    last = nc.scalar.activation(dispT[:, c, :], misc_b[:, c * N:(c + 1) * N], ACT.Exp,
                                                bias=neg_max_slot[:, c:c + 1], accum_out=disp_sum[:, c:c + 1])
                last.then_inc(dexp_ready, 1)

            def disp_high(b):
                act.wait_ge(disp_done, b + 1)
                wait(act, slotin_done, b)
                copy(disp_h[:, :, :].rearrange("p t e -> p (t e)"), misc_b[:, :]).then_inc(disph_ready, 1)

            def combT_high(b):
                act.wait_ge(combT_done, b + 1)
                copy(combT_h[:, bass.ds(b, 1), :, :].rearrange("p o c n -> p (o c n)"), misc_a[:, :]).then_inc(combTh_ready, 1)

            def slot_in_copy(b):
                act.wait_ge(slotin_done, b + 1)
                copy(slot_in[:, :, :, :, bass.ds(b, 1)].rearrange("p c e s o -> p (c e s o)"),
                     misc_b[:, :]).then_inc(slotin_ready, 1)

            act.wait_ge(small_loaded, 16 * 7)
            nc.scalar.activation(tanhs[:, :], gates[:, :], ACT.Tanh).then_inc(tanh_ready, 1)
            nc.scalar.preload_act_table_set("natural_log_exp_and_others")
            guess1(0)

            def wq_high(c):
                n = slice(c * INNER // 2, (c + 1) * INNER // 2)
                act.wait_ge(wq_loaded, 16 * (c + 1) if c else 32)
                copy(wq_h[:, :, n], wq_raw[:, :, n]).then_inc(wqh_ready, 1)

            ctxT_copy(0)
            ctxT_move(0)
            wq_high(0)
            xT_high(0)
            wq_high(1)
            act.wait_ge(zeros_ready, 4)
            proj_high(0, 0)
            proj_high(0, 1)
            act.wait_ge(b1T_done, 1)
            copy(b1T[:, :], attn_ps[0:H, 0:E]).then_inc(b1T_ready, 1)
            exps(0, 0)

            def first_prep(p):
                if p < 4:
                    act.wait_ge(wo_loaded, 16)
                    c = slice(p * PAIRS // 4, (p + 1) * PAIRS // 4)
                    copy(wo_h[:, c, :], wo_raw[:, c, :]).then_inc(woh_ready, 1)
                if p == 3:
                    act.wait_ge(muss_ready, 1)
                    guess(mu_nt[:, 2, :], mu_nt[:, 1, :], mu_nt[:, 0, :], mu_act, 1, LN_SHIFT).then_inc(muguess_ready, 1)
                if p == 6:
                    act.wait_ge(muunit_ready, 1)
                    copy(mu_h[:, :, :], mu_sq[:, :, :]).then_inc(muh_ready, 1)

            def step_loop(b, first, last):
                for p in range(PAIRS):
                    if not first:
                        if p == 4:
                            xn2T_high(b - 1)
                            guess3(b - 1)
                        if p == 5:
                            logits_scaled(b - 1)
                        if p == 7:
                            disp_high(b - 1)
                    if p < PAIRS - 2:
                        proj_high(b, p + 2)
                    elif not last:
                        proj_high(b + 1, p + 2 - PAIRS)
                    if not last and p == 1:
                        guess1(b + 1)
                    if not first:
                        if p == 3:
                            guess2(b - 1)
                        if p == 6:
                            disp_exp(b - 1)
                    if not last and p == 5:
                        ctxT_move(b + 1)
                        xT_high(b + 1)
                    probT_high(b, p)
                    if p < PAIRS - 1:
                        exps(b, p + 1)
                    elif not last:
                        exps(b + 1, 0)
                    if not last and p == 4:
                        ctxT_copy(b + 1)
                    if p > 0:
                        attn_high(b, p - 1)
                    elif not first:
                        attn_high(b - 1, PAIRS - 1)
                    if first:
                        first_prep(p)
                    else:
                        if p == 3:
                            square_sums(b - 1)
                        if p == 5:
                            comb_exp(b - 1)
                        if p == 7:
                            combT_high(b - 1)
                            slot_in_copy(b - 1)

            batches(act, nc.scalar, step_loop)
            attn_high(B - 1, PAIRS - 1)
            guess2(B - 1)
            square_sums(B - 1)
            guess3(B - 1)
            xn2T_high(B - 1)
            logits_scaled(B - 1)
            disp_exp(B - 1)
            comb_exp(B - 1)
            disp_high(B - 1)
            combT_high(B - 1)
            slot_in_copy(B - 1)

            for k in range(E // EQ):
                act.wait_ge(hid_done, k + 1)
                for i in range(EQ):
                    e = k * EQ + i
                    last = nc.scalar.activation(hidT[0:H, e, :], scores_ps[k % 2][0:H, i * SLOTS:(i + 1) * SLOTS], ACT.Gelu,
                                                bias=b1T[:, e:e + 1])
                last.then_inc(hid_ready, 1)
            for b in range(B):
                act.wait_ge(so_back[b % SR], 16 * (b // SR + 1))
                wait(act, mix_done, b - 1)
                copy(so_h[:, b % 2, :, :], so_rx[:, b % SR, :, :]).then_inc(soh_ready, 1)
                if b > 0:
                    act.wait_ge(out_ready, b)
                    act.dma_start(rows(out[b - 1, :, :], P), out_t[:, (b - 1) % 2, :, :]).then_inc(out_sent[(b - 1) % 2], 16)
            act.wait_ge(out_ready, B)
            act.dma_start(rows(out[B - 1, :, :], P), out_t[:, (B - 1) % 2, :, :]).then_inc(out_sent[(B - 1) % 2], 16)

        @block.vector
        def _(dve):
            V = nc.vector

            def split(dst_l, src, dst_h, scale=None):
                if scale is None:
                    return V.tensor_tensor(dst_l, src, dst_h.bitcast(F32), ALU.subtract)
                return V.scalar_tensor_tensor(dst_l, src, scale, dst_h.bitcast(F32), ALU.mult, ALU.subtract)

            def link(ins, chain, n):
                ins.then_inc(chain, 1)
                dve.wait_ge(chain, n)

            def hold():
                V.memset(pause[:, :], 0.0)

            def newton(t, chain, n):
                link(V.scalar_tensor_tensor(t[:, 3, :], t[:, 2, :], -0.5, t[:, 2, :], ALU.mult, ALU.mult), chain, n)
                link(V.tensor_tensor(t[:, 3, :], t[:, 3, :], t[:, 0, :], ALU.mult), chain, n + 1)
                return V.scalar_tensor_tensor(t[:, 4, :], t[:, 3, :], 1.5, t[:, 2, :], ALU.add, ALU.mult)

            NORM1 = 2 + 3
            FFN = 3 + 3 + 4 + 2

            def moments(tile_of, stats, mv, chain, n):
                for t in range(NT):
                    last = V.bn_stats(stats[:, t, :], tile_of(t))
                link(last, chain, n)
                hold()
                for t in range(NT):
                    last = V.bn_aggr(mv[:, t, :], stats[:, t, :])
                link(last, chain, n + 1)

            def x_tile(b, t):
                return x_all[:, bass.ds(b, 1), t, :].rearrange("p o d -> p (o d)")

            def norm1_stats(b, loaded):
                dve.wait_ge(loaded, 16)
                moments(lambda t: x_tile(b, t), stats1, mv1, norm1_chain, NORM1 * b + 1)
                V.tensor_scalar(nt1[:, 0, :], mv1[:, :, 1], 1.0, LN_EPS, ALU.mult, ALU.add).then_inc(var1_ready, 1)

            def norm1(b):
                dve.wait_ge(guess1_ready, b + 1)
                link(newton(nt1, norm1_chain, NORM1 * b + 3), norm1_chain, NORM1 * b + 5)
                wait(dve, xT_done, b)
                for t in range(NT):
                    last = V.tensor_scalar(xn[:, t, :], x_tile(b, t), mv1[:, t, 0:1], nt1[:, 4, t:t + 1],
                                           ALU.subtract, ALU.mult)
                last.then_inc(xn_ready, 1)

            def xT_low(b):
                dve.wait_ge(xTh_ready, b + 1)
                split(xT_l[:, :, :].rearrange("p c n -> p (c n)"), misc_a[:, :],
                      xT_h[:, :, :].rearrange("p c n -> p (c n)")).then_inc(xTl_ready, 1)

            def proj_low(b, p):
                g, r = 8 * b + p, p % 2
                dve.wait_ge(projh_ready, g + 1)
                split(q_l[:, r, :], proj_ps[:, 0:N], q_h[:, r, :], QK_SCALE)
                for h in range(2):
                    c = slice(h * HEAD, (h + 1) * HEAD)
                    m = slice(h * M, (h + 1) * M)
                    split(k_l[c, r, m], proj_ps[c, N:N + M], k_h[c, r, m])
                split(v_cols(v_l, p), proj_ps[0:M, N + M:N + M + P].rearrange("m (h d) -> m h d", h=2),
                      v_cols(v_h, p)).then_inc(projl_ready, 1)

            def maxima(b, p):
                g, r = 8 * b + p, p % 2
                dve.wait_ge(scores_done, g + 1)
                wait(dve, exp_done, g - 1)
                V.tensor_reduce(neg_max[:, r, :], scores_ps[r][:, 0:4 * M].rearrange("p (j m) -> p j m", m=M),
                                axis=AX.X, op=ALU.max, negate=True).then_inc(negmax_ready, 1)

            def probT_low(b, p):
                g, r = 8 * b + p, p % 2
                dve.wait_ge(pth_ready, g + 1)
                split(probT_l[:, r, :], probT_ps[r][0:M, :], probT_h[:, r, :]).then_inc(ptl_ready, 1)

            def attn_low(b, p):
                g = 8 * b + p
                dve.wait_ge(attnh_ready, g + 1)
                split(attn_l[:, p, :], attn_ps[:, 0:N], attn_h[:, p, :]).then_inc(attnl_ready, 1)

            def reciprocals(b, p):
                g, r = 8 * b + p, p % 2
                dve.wait_ge(exp_done, g + 1)
                wait(dve, prob_ready, g - 1)
                V.reciprocal(prob_rec[:, r, :], prob_sum[:, r, :]).then_inc(rec_ready, 1)

            def x1_stats(b):
                dve.wait_ge(y_done, b + 1)
                dve.wait_ge(xb_ready, b + 1)
                dve.wait_ge(tanh_ready, 1)
                xb = x_all[:, bass.ds(b, 1), :, :].rearrange("p o t d -> p (o t d)")
                ins = V.scalar_tensor_tensor(xb, misc_a[:, :], tanhs[:, 0:1], xb, ALU.mult, ALU.add)
                ins.then_inc(x1_ready, 1)
                dve.wait_ge(x1_ready, b + 1)
                hold()
                moments(lambda t: x_tile(b, t), stats2, mv2, ffn_chain, FFN * b + 1)
                V.tensor_scalar(nt2[:, 0, :], mv2[:, :, 1], 1.0 + LN_EPS, LN_EPS * LN_EPS, ALU.mult, ALU.add)\
                    .then_inc(var2_ready, 1)
                dve.wait_ge(small_loaded, 16 * 7)
                wait(dve, xn2l_ready, b)
                wait(dve, xn2T_done, b)
                for t in range(NT):
                    last = V.scalar_tensor_tensor(xn2[:, t, :], x_tile(b, t), mv2[:, t, 0:1], gamma[:, :],
                                                  ALU.subtract, ALU.mult)
                link(last, ffn_chain, FFN * b + 3)

            def x1_hat(b):
                dve.wait_ge(guess2_ready, b + 1)
                link(newton(nt2, ffn_chain, FFN * b + 4), ffn_chain, FFN * b + 6)
                for t in range(NT):
                    last = V.scalar_tensor_tensor(xn2[:, t, :], xn2[:, t, :], nt2[:, 4, t:t + 1], beta[:, :],
                                                  ALU.mult, ALU.add)
                last.then_inc(xn2_ready, 1)

            def guard_norm(b):
                dve.wait_ge(ss_ready, b + 1)
                V.tensor_scalar_max(nt3[:, 0, :], nt3[:, 5, :], NORM_EPS * NORM_EPS).then_inc(ssm_ready, 1)
                dve.wait_ge(xn2h_ready, b + 1)
                split(xn2_l[:, :, :], xn2[:, :, :], xn2_h[:, :, :]).then_inc(xn2l_ready, 1)

            def token_scale(b):
                dve.wait_ge(guess3_ready, b + 1)
                n = FFN * b + 7
                link(V.tensor_scalar_mul(nt3[:, 2, :], nt3[:, 2, :], float(2 ** (LN_SHIFT // 2))), ffn_chain, n)
                link(newton(nt3, ffn_chain, n + 1), ffn_chain, n + 3)
                wait(dve, logit_ready, b)
                V.tensor_scalar(nt3[:, 6, :], nt3[:, 4, :], scale_t[:, 0:1], None, ALU.mult).then_inc(rs_ready, 1)

            def xn2T_low(b):
                dve.wait_ge(xn2Th_ready, b + 1)
                split(xn2T_l[:, :, :].rearrange("p c n -> p (c n)"), misc_b[:, :],
                      xn2T_h[:, :, :].rearrange("p c n -> p (c n)")).then_inc(xn2Tl_ready, 1)

            def comb_max(b):
                dve.wait_ge(logit_ready, b + 1)
                V.tensor_reduce(neg_max_all[:, :], logit[:, :, :], axis=AX.X, op=ALU.max,
                                negate=True).then_inc(allmax_ready, 1)

            def disp_max(b):
                dve.wait_ge(logitT_done, b + 1)
                V.tensor_reduce(neg_max_slot[:, :], misc_b[:, :].rearrange("p (c n) -> p c n", c=EC), axis=AX.X, op=ALU.max,
                                negate=True).then_inc(slotmax_ready, 1)

            def comb_norm(b):
                dve.wait_ge(cexp_ready, b + 1)
                link(V.reciprocal(comb_rec[:, :], comb_sum[:, :]), ffn_chain, FFN * b + 12)
                for t in range(NT):
                    last = V.tensor_scalar(comb[:, t, :], comb[:, t, :], comb_rec[:, t:t + 1], None, ALU.mult)
                last.then_inc(comb_ready, 1)

            def disp_norm(b):
                dve.wait_ge(dexp_ready, b + 1)
                link(V.reciprocal(disp_rec[:, :], disp_sum[:, :]), ffn_chain, FFN * b + 11)
                for c in range(EC):
                    last = V.tensor_scalar(dispT[:, c, :], dispT[:, c, :], disp_rec[:, c:c + 1], None, ALU.mult)
                last.then_inc(dispT_ready, 1)

            def disp_low(b):
                dve.wait_ge(disph_ready, b + 1)
                split(disp_l[:, :, :].rearrange("p t e -> p (t e)"), misc_b[:, :],
                      disp_h[:, :, :].rearrange("p t e -> p (t e)")).then_inc(displ_ready, 1)

            def combT_low(b):
                dve.wait_ge(combTh_ready, b + 1)
                ct = [c[:, bass.ds(b, 1), :, :].rearrange("p o c n -> p (o c n)") for c in (combT_h, combT_l)]
                split(ct[1], misc_a[:, :], ct[0]).then_inc(combTl_ready, 1)

            for t in (k_h, k_l, v_h, v_l):
                flat = t[:, :, :].rearrange("p r m -> p (r m)") if len(t.shape) == 3 else \
                    t[:, :, :, :].rearrange("p r h m -> p (r h m)")
                V.memset(flat.bitcast(F32), 0.0).then_inc(zeros_ready, 1)
            norm1_stats(0, x0_loaded)
            norm1(0)

            def wq_low(c):
                n = slice(c * INNER // 2, (c + 1) * INNER // 2)
                dve.wait_ge(wqh_ready, c + 1)
                split(wq_l[:, :, n], wq_raw[:, :, n], wq_h[:, :, n]).then_inc(wql_ready, 1)

            wq_low(0)
            xT_low(0)
            wq_low(1)
            dve.wait_ge(tanh_ready, 1)
            V.tensor_scalar(bo_t[:, :], bo_t[:, :], tanhs[:, 0:1], None, ALU.mult).then_inc(bo_ready, 1)
            proj_low(0, 0)
            maxima(0, 0)
            proj_low(0, 1)
            reciprocals(0, 0)

            def first_prep(p):
                if p == 2:
                    dve.wait_ge(munorm_done, 1)
                    V.tensor_scalar_max(mu_nt[:, 0, :], misc_a[:, 0:ES], NORM_EPS * NORM_EPS).then_inc(muss_ready, 1)
                if p == 4:
                    dve.wait_ge(muguess_ready, 1)
                    link(V.tensor_scalar_mul(mu_nt[:, 2, :], mu_nt[:, 2, :], float(2 ** (LN_SHIFT // 2))), mu_chain, 1)
                    newton(mu_nt, mu_chain, 2).then_inc(murn_ready, 1)
                if p == 7:
                    dve.wait_ge(muh_ready, 1)
                    split(mu_l[:, :, :], mu_sq[:, :, :], mu_h[:, :, :]).then_inc(mul_ready, 1)

            def step_loop(b, first, last):
                for p in range(PAIRS):
                    if not first:
                        if p == 4:
                            xn2T_low(b - 1)
                        if p == 6:
                            disp_max(b - 1)
                        if p == 7:
                            disp_low(b - 1)
                    if p < PAIRS - 1:
                        maxima(b, p + 1)
                    elif not last:
                        maxima(b + 1, 0)
                    if p < PAIRS - 2:
                        proj_low(b, p + 2)
                    elif not last:
                        proj_low(b + 1, p + 2 - PAIRS)
                    if not last and p == 5:
                        xT_low(b + 1)
                    if not first:
                        if p == 3:
                            x1_hat(b - 1)
                        if p == 6:
                            disp_norm(b - 1)
                    probT_low(b, p)
                    if p < PAIRS - 1:
                        reciprocals(b, p + 1)
                    elif not last:
                        reciprocals(b + 1, 0)
                    if p > 0:
                        attn_low(b, p - 1)
                    elif not first:
                        attn_low(b - 1, PAIRS - 1)
                    if first:
                        first_prep(p)
                    else:
                        if p == 2:
                            x1_stats(b - 1)
                        if p == 3:
                            guard_norm(b - 1)
                        if p == 4:
                            token_scale(b - 1)
                        if p == 5:
                            comb_max(b - 1)
                        if p == 6:
                            comb_norm(b - 1)
                        if p == 7:
                            combT_low(b - 1)
                    if not last and p == 0:
                        norm1_stats(b + 1, x_loaded)
                    if not last and p == 1:
                        norm1(b + 1)

            batches(dve, nc.vector, step_loop)
            attn_low(B - 1, PAIRS - 1)
            x1_stats(B - 1)
            x1_hat(B - 1)
            guard_norm(B - 1)
            token_scale(B - 1)
            xn2T_low(B - 1)
            comb_max(B - 1)
            disp_max(B - 1)
            disp_norm(B - 1)
            comb_norm(B - 1)
            disp_low(B - 1)
            combT_low(B - 1)

            dve.wait_ge(attn_done, B * PAIRS)
            dve.wait_ge(mul_ready, 1)
            V.memset(hidT[H:H + 1, :, :], 1.0).then_inc(ones_ready, 1)
            for j in range(E // 2):
                dve.wait_ge(so_done, j + 1)
                if j >= SR:
                    dve.wait_ge(so_sent[j % SR], 16)
                V.tensor_copy(so_tx[:, j % SR, :, :].rearrange("p e d -> p (e d)"), probT_ps[j % 2][:, :]).then_inc(so_ready, 1)

            def mix_out(b):
                dve.wait_ge(mix_done, b + 1)
                if b >= 2:
                    dve.wait_ge(out_sent[b % 2], 16 * (b // 2))
                V.scalar_tensor_tensor(out_t[:, b % 2, :, :].rearrange("p t d -> p (t d)"), scores_ps[b % 2][:, :],
                                       tanhs[:, 1:2], x_all[:, b, :, :].rearrange("p t d -> p (t d)"),
                                       ALU.mult, ALU.add).then_inc(out_ready, 1)

            for b in range(B):
                dve.wait_ge(soh_ready, b + 1)
                wait(dve, mix_done, b - 1)
                split(so_l[:, b % 2, :, :], so_rx[:, b % SR, :, :], so_h[:, b % 2, :, :]).then_inc(sol_ready, 1)
                if b > 0:
                    mix_out(b - 1)
            mix_out(B - 1)

        @block.tensor
        def _(pe):
            def product(o, terms, start=True, stop=True):
                n = 3 * len(terms)
                i = 0
                for ah, al, bh, bl in terms:
                    for lhs, rhs in ((ah, bh), (ah, bl), (al, bh)):
                        last = nc.tensor.matmul(o, lhs, rhs, start=start and i == 0, stop=stop and i == n - 1)
                        i += 1
                return last

            def xT(b, first):
                pe.wait_ge(xn_ready, b + 1)
                wait(pe, logit_ready, b - 1)
                if first:
                    pe.wait_ge(ctxT_staged, b + 1)
                for t in range(NT):
                    for c in range(DC):
                        last = nc.tensor.transpose(misc_a[:, c * N + t * P:c * N + (t + 1) * P],
                                                   xn[:, t, c * P:(c + 1) * P], ident[:, :])
                last.then_inc(xT_done, 1)

            def transpose_ctx(b, first=False):
                pe.wait_ge(ctx_loaded, 16 * (b + 1))
                wait(pe, x1_ready, b - 1)
                if first:
                    pe.wait_ge(muss_ready, 1)
                nc.tensor.transpose(misc_a[:, 0:M], ctx_in[:, :], ident[0:M, 0:M]).then_inc(ctxT_done, 1)

            def project(b, p):
                g = 8 * b + p
                if p == 0:
                    pe.wait_ge(xTl_ready, b + 1)
                    pe.wait_ge(ctxT_ready, b + 1)
                wait(pe, projl_ready, g)
                c = slice(p * P, (p + 1) * P)
                product(proj_ps[:, 0:N], [(wq_h[:, k, c], wq_l[:, k, c], xT_h[:, k, :], xT_l[:, k, :]) for k in range(DC)])
                nc.tensor.matmul(proj_ps[:, N:N + M], wk[:, c], ctxT[:, :], start=True, stop=True)
                nc.tensor.matmul(proj_ps[0:M, N + M:N + M + P], ctxT[:, :], wv[:, c], start=True, stop=True)\
                    .then_inc(proj_done, 1)

            def score(b, p):
                g, r = 8 * b + p, p % 2
                pe.wait_ge(projl_ready, g + 1)
                wait(pe, exp_done, g - 1)
                for t in range(NT):
                    c = slice(t * P, (t + 1) * P)
                    last = product(scores_ps[r][:, t * K2:(t + 1) * K2],
                                   [(q_h[:, r, c], q_l[:, r, c], k_h[:, r, :], k_l[:, r, :])])
                last.then_inc(scores_done, 1)

            def transpose_prob(b, p):
                g, r = 8 * b + p, p % 2
                pe.wait_ge(prob_ready, g + 1)
                wait(pe, ptl_ready, g - 1)
                for h in range(2):
                    for t in range(NT):
                        o = h * N + t * P
                        last = nc.tensor.transpose(probT_ps[r][0:M, o:o + P], prob[:, r, t, h, :], ident[:, :])
                last.then_inc(probT_done, 1)

            def attend(b, p):
                g, r, v = 8 * b + p, p % 2, p % VR
                pe.wait_ge(ptl_ready, g + 1)
                wait(pe, attnl_ready, g)
                product(attn_ps[:, 0:N], [(v_h[:, v, h, :], v_l[:, v, h, :], probT_h[:, r, h * N:(h + 1) * N],
                                           probT_l[:, r, h * N:(h + 1) * N]) for h in range(2)]).then_inc(attn_done, 1)

            def output_projection(b):
                pe.wait_ge(attnl_ready, 8 * b + 8)
                pe.wait_ge(wol_ready, 4)
                wait(pe, combTl_ready, b)
                for t in range(NT):
                    c = slice(t * P, (t + 1) * P)
                    last = product(misc_a[:, t * D:(t + 1) * D],
                                   [(attn_h[:, k, c], attn_l[:, k, c], wo_h[:, k, :], wo_l[:, k, :]) for k in range(PAIRS)])
                last.then_inc(y_done, 1)

            def transpose_xn2(b):
                pe.wait_ge(xn2_ready, b + 1)
                wait(pe, slotin_ready, b)
                for t in range(NT):
                    for c in range(DC):
                        last = nc.tensor.transpose(misc_b[:, c * N + t * P:c * N + (t + 1) * P],
                                                   xn2[:, t, c * P:(c + 1) * P], ident[:, :])
                last.then_inc(xn2T_done, 1)

            def logits(b, last_batch):
                pe.wait_ge(xn2Tl_ready, b + 1)
                if last_batch:
                    pe.wait_ge(x1_ready, b + 1)
                else:
                    pe.wait_ge(ctxT_staged, b + 3)
                pe.wait_ge(mul_ready, 1)
                for t in range(NT):
                    c = slice(t * P, (t + 1) * P)
                    last = product(misc_a[:, t * ES:(t + 1) * ES],
                                   [(xn2T_h[:, k, c], xn2T_l[:, k, c], mu_h[:, k, :], mu_l[:, k, :]) for k in range(DC)])
                last.then_inc(logits_done, 1)

            def transpose_logits(b):
                pe.wait_ge(logit_ready, b + 1)
                for c in range(EC):
                    for t in range(NT):
                        last = nc.tensor.transpose(misc_b[:, c * N + t * P:c * N + (t + 1) * P],
                                                   logit[:, t, c * P:(c + 1) * P], ident[:, :])
                last.then_inc(logitT_done, 1)

            def transpose_disp(b):
                pe.wait_ge(dispT_ready, b + 1)
                for t in range(NT):
                    for c in range(EC):
                        last = nc.tensor.transpose(misc_b[:, t * ES + c * P:t * ES + (c + 1) * P],
                                                   dispT[:, c, t * P:(t + 1) * P], ident[:, :])
                last.then_inc(disp_done, 1)

            def transpose_comb(b, last_batch):
                pe.wait_ge(comb_ready, b + 1)
                if not last_batch:
                    pe.wait_ge(xTl_ready, b + 3)
                for c in range(EC):
                    for t in range(NT):
                        last = nc.tensor.transpose(misc_a[:, c * N + t * P:c * N + (t + 1) * P],
                                                   comb[:, t, c * P:(c + 1) * P], ident[:, :])
                last.then_inc(combT_done, 1)

            def slot_inputs(b):
                pe.wait_ge(displ_ready, b + 1)
                pe.wait_ge(xn2l_ready, b + 1)
                for c in range(DC):
                    d = slice(c * P, (c + 1) * P)
                    last = product(misc_b[:, c * ES:(c + 1) * ES],
                                   [(xn2_h[:, t, d], xn2_l[:, t, d], disp_h[:, t, :], disp_l[:, t, :]) for t in range(NT)])
                last.then_inc(slotin_done, 1)

            pe.wait_ge(ident_ready, 1)
            transpose_ctx(0)
            xT(0, True)
            pe.wait_ge(small_loaded, 16 * 7)
            nc.tensor.transpose(attn_ps[0:H, 0:E], b1_in[:, :], ident[0:E, 0:E]).then_inc(b1T_done, 1)
            pe.wait_ge(wkv_loaded, 32)
            pe.wait_ge(wql_ready, 2)
            project(0, 0)
            project(0, 1)
            score(0, 0)

            def step_loop(b, first, last):
                for p in range(PAIRS):
                    if p < PAIRS - 2:
                        project(b, p + 2)
                    elif not last:
                        project(b + 1, p + 2 - PAIRS)
                    if p < PAIRS - 1:
                        score(b, p + 1)
                    elif not last:
                        score(b + 1, 0)
                    if not last and p == 4:
                        transpose_ctx(b + 1, first)
                    if not last and p == 5:
                        xT(b + 1, first)
                    transpose_prob(b, p)
                    if p > 0:
                        attend(b, p - 1)
                    elif not first:
                        attend(b - 1, PAIRS - 1)
                    if first:
                        if p == 1:
                            pe.wait_ge(musq_ready, 1)
                            for c in range(DC):
                                mm = nc.tensor.matmul(misc_a[:, 0:ES], ones[:, :], mu_sq[:, c, :],
                                                      start=c == 0, stop=c == DC - 1)
                            mm.then_inc(munorm_done, 1)
                        continue
                    if p == 1:
                        output_projection(b - 1)
                    if p == 3:
                        transpose_xn2(b - 1)
                    if p == 4:
                        logits(b - 1, last)
                    if p == 5:
                        transpose_logits(b - 1)
                    if p == 6:
                        transpose_disp(b - 1)
                    if p == 7:
                        transpose_comb(b - 1, last)
                        slot_inputs(b - 1)

            batches(pe, nc.tensor, step_loop)
            attend(B - 1, PAIRS - 1)
            output_projection(B - 1)
            transpose_xn2(B - 1)
            logits(B - 1, True)
            transpose_logits(B - 1)
            transpose_disp(B - 1)
            transpose_comb(B - 1, True)
            slot_inputs(B - 1)

            pe.wait_ge(exp_loaded, 48)
            pe.wait_ge(slotin_ready, B)
            for k in range(E // EQ):
                if k >= 2:
                    pe.wait_ge(hid_ready, k - 1)
                for i in range(EQ):
                    e = k * EQ + i
                    for c in range(DC):
                        last = nc.tensor.matmul(scores_ps[k % 2][0:H, i * SLOTS:(i + 1) * SLOTS], w1_t[:, e, c, :],
                                                slot_in[:, c, e, :, :].rearrange("p s b -> p (s b)"),
                                                start=c == 0, stop=c == DC - 1)
                last.then_inc(hid_done, 1)
            pe.wait_ge(ones_ready, 1)
            for j in range(E // 2):
                pe.wait_ge(hid_ready, 2 * j // EQ + 1)
                if j >= 2:
                    pe.wait_ge(so_ready, j - 1)
                for i in range(2):
                    last = nc.tensor.matmul(probT_ps[j % 2][:, i * D:(i + 1) * D], hidT[:, 2 * j + i, :],
                                            w2_t[:, 2 * j + i, :], start=True, stop=True)
                last.then_inc(so_done, 1)
            for b in range(B):
                pe.wait_ge(sol_ready, b + 1)
                if b >= 2:
                    pe.wait_ge(out_ready, b - 1)
                for t in range(NT):
                    c = slice(t * P, (t + 1) * P)
                    last = product(scores_ps[b % 2][:, t * D:(t + 1) * D],
                                   [(combT_h[:, b, k, c], combT_l[:, b, k, c], so_h[:, b % 2, k, :], so_l[:, b % 2, k, :])
                                    for k in range(EC)])
                last.then_inc(mix_done, 1)


_INS = ['x', 'ctx_512', 'g_xattn', 'g_ffn', 'L0_xattn_Wq', 'L0_xattn_Wk', 'L0_xattn_Wv', 'L0_xattn_Wo', 'L0_xattn_bo',
        'L0_ffn_ln_gamma', 'L0_ffn_ln_beta', 'L0_ffn_mu', 'L0_ffn_scale', 'L0_ffn_w1', 'L0_ffn_b1', 'L0_ffn_w2', 'L0_ffn_b2']


def kernel(**inputs):
    import concourse.bacc as _bacc
    from concourse.bass_utils import run_bass_kernel_spmd as _run

    nc = _bacc.Bacc("TRN2", target_bir_lowering=False, num_devices=1)
    arrays, args = {}, []
    for name in _INS:
        a = np.ascontiguousarray(inputs[name])
        arrays[f"in_{name}_dram"] = a
        args.append(nc.dram_tensor(f"in_{name}_dram", a.shape, mybir.dt.from_np(a.dtype), kind="ExternalInput").ap())
    shape = inputs['x'].shape
    args.append(nc.dram_tensor("out_0_dram", shape, F32, kind="ExternalOutput").ap())
    flamingo_layer(nc, *args)
    r = _run(nc, [arrays], core_ids=[0])
    return r.results[0]["out_0_dram"]
```

```python
from contextlib import ExitStack

import numpy as np
import concourse.bass as bass
from concourse import mybir

F32 = mybir.dt.float32
F32R = mybir.dt.float32r
ALU = mybir.AluOpType
ACT = mybir.ActivationFunctionType
AX = mybir.AxisListType

P = 128
HEAD = 64
LN_EPS = 1e-5
NORM_EPS = 1e-12
LN_SHIFT = 20



def rows(ap, p):
    return ap.rearrange("(t p) d -> p t d", p=p)


def flamingo_layer(nc, x, ctx_kv, g_xattn, g_ffn, Wq, Wk, Wv, Wo, bo, ln_gamma, ln_beta, mu, scale,
                   w1, b1, w2, b2, out):
    B, N, D = x.shape
    M, KV = ctx_kv.shape[1:]
    INNER = Wq.shape[1]
    PAIRS = INNER // P
    NT = N // P
    DC = D // P
    _, E, S = mu.shape
    ES = E * S
    EC = ES // P
    H = w1.shape[2]
    assert KV == P and D == 2 * P and N == 2 * P and ES == 2 * P and PAIRS % 4 == 0 and 4 * M <= 512
    K2 = 2 * M
    QK_SCALE = float(HEAD) ** -0.5
    EQ = 4
    SLOTS = S * B
    AHEAD = 3
    AHEAD_S = AHEAD - 1
    QR = 4
    VR = 8
    SR = 4
    MR = 4

    slot_out_dram = nc.dram_tensor("slot_out", (E, S, B, D), F32, kind="Internal").ap()

    with ExitStack() as top:
        def sb(stack, name, shape, dt=F32):
            return stack.enter_context(nc.sbuf_tensor(name, shape, dt))

        def sem(name):
            return top.enter_context(nc.semaphore(name))

        def bank(name):
            return top.enter_context(nc.psum_tensor(name, [P, 512], F32))

        scores_ps = [bank(f"scores_ps{i}") for i in range(2)]
        proj_ps = [bank(f"proj_ps{i}") for i in range(2)]
        probT_ps = bank("probT_ps")
        attn_ps = bank("attn_ps")
        misc_a = bank("misc_a")
        misc_b = bank("misc_b")

        x_all = sb(top, "x_all", [P, B, NT, D])
        wo_h = sb(top, "wo_h", [P, PAIRS, D], F32R)
        wo_l = sb(top, "wo_l", [P, PAIRS, D], F32R)
        mu_h = sb(top, "mu_h", [P, DC, ES], F32R)
        mu_l = sb(top, "mu_l", [P, DC, ES], F32R)
        combT_h = sb(top, "combT_h", [P, B, EC, N], F32R)
        combT_l = sb(top, "combT_l", [P, B, EC, N], F32R)
        slot_in = sb(top, "slot_in", [P, DC, E, S, B])
        attn_h = sb(top, "attn_h", [P, PAIRS, N], F32R)
        attn_l = sb(top, "attn_l", [P, PAIRS, N], F32R)
        xn2 = sb(top, "xn2", [P, NT, D])
        xn2_h = sb(top, "xn2_h", [P, NT, D], F32R)
        xn2_l = sb(top, "xn2_l", [P, NT, D], F32R)
        xn2T_h = sb(top, "xn2T_h", [P, DC, N], F32R)
        xn2T_l = sb(top, "xn2T_l", [P, DC, N], F32R)
        logit = sb(top, "logit", [P, NT, ES])
        dispT = sb(top, "dispT", [P, EC, N])
        disp_h = sb(top, "disp_h", [P, NT, ES], F32R)
        disp_l = sb(top, "disp_l", [P, NT, ES], F32R)
        comb = sb(top, "comb", [P, NT, ES])
        squares = sb(top, "squares", [P, NT, D])
        gamma = sb(top, "gamma", [P, D])
        beta = sb(top, "beta", [P, D])
        bo_t = sb(top, "bo_t", [P, D])
        ident = sb(top, "ident", [P, P])
        b1_in = sb(top, "b1_in", [E, H])
        b1T = sb(top, "b1T", [H, E])
        gates = sb(top, "gates", [P, 2])
        tanhs = sb(top, "tanhs", [P, 2])
        scale_t = sb(top, "scale_t", [P, 1])
        pause = sb(top, "pause", [P, 1])
        stats1 = sb(top, "stats1", [P, NT, 6])
        mv1 = sb(top, "mv1", [P, NT, 2])
        nt1 = sb(top, "nt1", [P, 5, NT])
        stats2 = sb(top, "stats2", [P, NT, 6])
        mv2 = sb(top, "mv2", [P, NT, 2])
        nt2 = sb(top, "nt2", [P, 5, NT])
        nt3 = sb(top, "nt3", [P, 7, NT])
        neg_max_slot = sb(top, "neg_max_slot", [P, EC])
        neg_max_all = sb(top, "neg_max_all", [P, NT])
        disp_sum = sb(top, "disp_sum", [P, EC])
        disp_rec = sb(top, "disp_rec", [P, EC])
        comb_sum = sb(top, "comb_sum", [P, NT])
        comb_rec = sb(top, "comb_rec", [P, NT])
        wq_raw = slot_in[:, :, :, :, :].rearrange("p c e s b -> p (c e s b)")[:, 0:DC * INNER]\
            .rearrange("p (c n) -> p c n", c=DC)
        wo_raw = slot_in[:, :, :, :, :].rearrange("p c e s b -> p (c e s b)")[:, DC * INNER:DC * INNER + PAIRS * D]\
            .rearrange("p (c n) -> p c n", c=PAIRS)

        with ExitStack() as attention:
            wq_h = sb(attention, "wq_h", [P, DC, INNER], F32R)
            wq_l = sb(attention, "wq_l", [P, DC, INNER], F32R)
            wk = sb(attention, "wk", [P, INNER])
            wv = sb(attention, "wv", [P, INNER])
            ctx_in = sb(attention, "ctx_in", [M, KV])
            ctxT = sb(attention, "ctxT", [P, M])
            ctxT_next = sb(attention, "ctxT_next", [P, M])
            xn = sb(attention, "xn", [P, NT, D])
            xT_h = sb(attention, "xT_h", [P, DC, N], F32R)
            xT_l = sb(attention, "xT_l", [P, DC, N], F32R)
            q_h = sb(attention, "q_h", [P, QR, N], F32R)
            q_l = sb(attention, "q_l", [P, QR, N], F32R)
            k_h = sb(attention, "k_h", [P, QR, K2], F32R)
            k_l = sb(attention, "k_l", [P, QR, K2], F32R)
            v_h = sb(attention, "v_h", [M, VR, 2, P], F32R)
            v_l = sb(attention, "v_l", [M, VR, 2, P], F32R)
            prob = sb(attention, "prob", [P, 2, NT, 2, M])
            probT_h = sb(attention, "probT_h", [M, 2, 2 * N], F32R)
            probT_l = sb(attention, "probT_l", [M, 2, 2 * N], F32R)
            neg_max = sb(attention, "neg_max", [P, 2, NT * 2])
            prob_sum = sb(attention, "prob_sum", [P, 2, NT * 2])
            prob_rec = sb(attention, "prob_rec", [P, 2, NT * 2])
            mu_raw, mu_sq = comb, logit
            mu_nt = sb(attention, "mu_nt", [P, 5, ES])
            ones = sb(attention, "ones", [P, P])

        with ExitStack() as experts:
            w1_t = sb(experts, "w1_t", [P, E, DC, H])
            w2_t = sb(experts, "w2_t", [H + 1, E, D])
            hidT = sb(experts, "hidT", [H + 1, E, SLOTS])
            so_tx = sb(experts, "so_tx", [P, SR, 2, D])
            so_rx = sb(experts, "so_rx", [P, B, EC, D])
            so_h = sb(experts, "so_h", [P, MR, EC, D], F32R)
            so_l = sb(experts, "so_l", [P, MR, EC, D], F32R)
            out_t = sb(experts, "out_t", [P, MR, NT, D])

        x0_loaded, x_loaded, ctx_loaded = sem("x0_loaded"), sem("x_loaded"), sem("ctx_loaded")
        wq_loaded, wkv_loaded, wo_loaded = [sem(f"wq_loaded{i}") for i in range(2)], sem("wkv_loaded"), sem("wo_loaded")
        gates_loaded, small_loaded, mu_loaded, exp_loaded = sem("gates_loaded"), sem("small_loaded"), sem("mu_loaded"), sem("exp_loaded")
        consts, zeros_ready, ident_ready, tanh_ready, bo_ready = sem("consts"), sem("zeros_ready"), sem("ident_ready"), sem("tanh_ready"), sem("bo_ready")
        wqh_ready, wql_ready = sem("wqh_ready"), sem("wql_ready")
        woh_ready, wol_ready = sem("woh_ready"), sem("wol_ready")
        musq_ready, munorm_done, muss_ready = sem("musq_ready"), sem("munorm_done"), sem("muss_ready")
        muguess_ready, murn_ready, muunit_ready = sem("muguess_ready"), sem("murn_ready"), sem("muunit_ready")
        b1T_done, b1T_ready = sem("b1T_done"), sem("b1T_ready")
        muh_ready, mul_ready, mu_chain, mu_act = sem("muh_ready"), sem("mul_ready"), sem("mu_chain"), sem("mu_act")
        var1_ready, guess1_ready, xn_ready = sem("var1_ready"), sem("guess1_ready"), sem("xn_ready")
        xT_done, xTh_ready, xTl_ready = sem("xT_done"), sem("xTh_ready"), sem("xTl_ready")
        ctxT_done, ctxT_staged, ctxT_ready = sem("ctxT_done"), sem("ctxT_staged"), sem("ctxT_ready")
        norm1_chain, act_chain1 = sem("norm1_chain"), sem("act_chain1")
        proj_done, projh_ready, projl_ready = sem("proj_done"), sem("projh_ready"), sem("projl_ready")
        scores_done, negmax_ready, exp_done = sem("scores_done"), sem("negmax_ready"), sem("exp_done")
        rec_ready, prob_ready, probT_done = sem("rec_ready"), sem("prob_ready"), sem("probT_done")
        pth_ready, ptl_ready = sem("pth_ready"), sem("ptl_ready")
        attn_done, attnh_ready, attnl_ready = sem("attn_done"), sem("attnh_ready"), sem("attnl_ready")
        xb_ready, y_done, x1_ready = sem("xb_ready"), sem("y_done"), sem("x1_ready")
        var2_ready, guess2_ready, xn2_ready = sem("var2_ready"), sem("guess2_ready"), sem("xn2_ready")
        ss_ready, ssm_ready, guess3_ready, rs_ready = sem("ss_ready"), sem("ssm_ready"), sem("guess3_ready"), sem("rs_ready")
        xn2h_ready, xn2l_ready = sem("xn2h_ready"), sem("xn2l_ready")
        xn2T_done, xn2Th_ready, xn2Tl_ready = sem("xn2T_done"), sem("xn2Th_ready"), sem("xn2Tl_ready")
        logits_done, logit_ready = sem("logits_done"), sem("logit_ready")
        logitT_done, slotmax_ready, allmax_ready = sem("logitT_done"), sem("slotmax_ready"), sem("allmax_ready")
        dexp_ready, cexp_ready, dispT_ready, disp_done = sem("dexp_ready"), sem("cexp_ready"), sem("dispT_ready"), sem("disp_done")
        disph_ready, displ_ready = sem("disph_ready"), sem("displ_ready")
        comb_ready, combT_done, combTh_ready, combTl_ready = (
            sem("comb_ready"), sem("combT_done"), sem("combTh_ready"), sem("combTl_ready"))
        slotin_done, slotin_ready = sem("slotin_done"), sem("slotin_ready")
        ffn_chain, act_chain2, act_chain3 = sem("ffn_chain"), sem("act_chain2"), sem("act_chain3")
        ones_ready, hid_done, hid_ready = sem("ones_ready"), sem("hid_done"), sem("hid_ready")
        so_done, so_ready = sem("so_done"), sem("so_ready")
        so_sent = [sem(f"so_sent{i}") for i in range(SR)]
        so_back = [sem(f"so_back{i}") for i in range(B)]
        soh_ready, sol_ready, mix_done, out_ready = sem("soh_ready"), sem("sol_ready"), sem("mix_done"), sem("out_ready")
        out_sent = [sem(f"out_sent{i}") for i in range(MR)]

        def wait(eng, s, n):
            if isinstance(n, int) and n <= 0:
                return
            eng.wait_ge(s, n)

        def near(stage, b, p, lag, first, last):
            if p + lag >= PAIRS:
                if not last:
                    stage(b + 1, p + lag - PAIRS)
            elif p + lag < 0:
                if not first:
                    stage(b - 1, p + lag + PAIRS)
            else:
                stage(b, p + lag)

        def v_cols(v, p):
            blocks = v[:, p % VR, :, :].rearrange("m h (k d) -> m (h k) d", d=HEAD)
            return blocks[:, 0:4:3, :]

        def batches(nc_eng, body):
            body(0, True, False)
            body(1, False, False)
            with nc_eng.Fori(2, B - 1) as b:
                body(b, False, False)
            body(B - 1, False, True)

        block = top.enter_context(nc.Block())

        @block.sync
        def _(sp):
            sp.dma_start(x_all[:, 0, :, :], rows(x[0, :, :], P)).then_inc(x0_loaded, 16)
            sp.dma_start(gates[:, 0:1], g_xattn.partition_broadcast(P)).then_inc(gates_loaded, 16)
            sp.dma_start(gates[:, 1:2], g_ffn.partition_broadcast(P)).then_inc(gates_loaded, 16)
            sp.dma_start(ctx_in[:, :], ctx_kv[0, :, :]).then_inc(ctx_loaded, 16)
            sp.dma_start(wk[:, :], Wk).then_inc(wkv_loaded, 16)
            sp.dma_start(wv[:, :], Wv).then_inc(wkv_loaded, 16)
            sp.dma_start(x_all[:, 1:B, :, :], x[1:B, :, :].rearrange("b (t p) d -> p b t d", p=P)).then_inc(x_loaded, 16)
            sp.dma_start(wo_raw, rows(Wo, P)).then_inc(wo_loaded, 16)
            sp.dma_start(mu_raw[:, :, :], mu.rearrange("(c p) e s -> p c (e s)", p=P)).then_inc(mu_loaded, 16)
            with nc.sync.Fori(1, B) as b:
                sp.wait_ge(ctxT_done, b)
                sp.dma_start(ctx_in[:, :], ctx_kv[bass.ds(b, 1), :, :].rearrange("o m k -> (o m) k")).then_inc(ctx_loaded, 16)
            sp.wait_ge(attn_done, B * PAIRS)
            sp.wait_ge(mul_ready, 1)
            sp.dma_start(w1_t[:, :, :, :], w1.rearrange("e (c p) h -> p e c h", p=P)).then_inc(exp_loaded, 16)
            sp.dma_start(w2_t[0:H, :, :], w2.rearrange("e h d -> h e d")).then_inc(exp_loaded, 16)
            sp.dma_start(w2_t[H:H + 1, :, :], b2.rearrange("(o e) d -> o e d", o=1)).then_inc(exp_loaded, 16)
            for j in range(E // 2):
                sp.wait_ge(so_ready, j + 1)
                sp.dma_start(slot_out_dram[2 * j:2 * j + 2, :, :, :].rearrange("e s b d -> (s b) e d"),
                             so_tx[:, j % SR, :, :]).then_inc(so_sent[j % SR], 16)
            for s in so_sent:
                sp.wait_ge(s, 16 * (E // 2 // SR))
            for b in range(B):
                sp.dma_start(so_rx[:, b, :, :],
                             slot_out_dram[:, :, b, :].rearrange("(c e) s d -> (e s) c d", c=EC)).then_inc(so_back[b], 16)
            for b in range(B):
                sp.wait_ge(out_ready, b + 1)
                sp.dma_start(rows(out[b, :, :], P), out_t[:, b % MR, :, :]).then_inc(out_sent[b % MR], 16)
            for s in out_sent:
                sp.wait_ge(s, 16 * (B // MR))

        @block.gpsimd
        def _(pool):
            nc.gpsimd.memset(ident[:, :], 0.0).then_inc(consts, 1)
            nc.gpsimd.memset(ones[:, :], 1.0).then_inc(consts, 1)
            pool.wait_ge(consts, 2)
            pool.affine_select(out=ident[:, :], in_=ident[:, :], compare_op=ALU.not_equal, fill=1.0,
                               base=0, pattern=[[-1, P]], channel_multiplier=1).then_inc(ident_ready, 1)
            for t in (v_h, v_l):
                nc.gpsimd.memset(t[:, :, :, :].rearrange("p r h m -> p (r h m)").bitcast(F32), 0.0).then_inc(zeros_ready, 1)
            pool.dma_start(bo_t[:, :], bo.partition_broadcast(P)).then_inc(small_loaded, 16)
            pool.dma_start(scale_t[:, :], scale.partition_broadcast(P)).then_inc(small_loaded, 16)
            pool.dma_start(gamma[:, :], ln_gamma.partition_broadcast(P)).then_inc(small_loaded, 16)
            pool.dma_start(beta[:, :], ln_beta.partition_broadcast(P)).then_inc(small_loaded, 16)
            pool.dma_start(b1_in[:, :], b1).then_inc(small_loaded, 16)

            def normalise(b, p):
                g = 8 * b + p
                r = p % 2
                pool.wait_ge(exp_done, g + 1)
                pool.wait_ge(rec_ready, g + 1)
                pr = prob[:, r, :, :, :].rearrange("p t h m -> p (t h) m")
                nc.gpsimd.tensor_tensor(pr, pr, prob_rec[:, r, :].unsqueeze(2).broadcast_to([P, NT * 2, M]),
                                        ALU.mult).then_inc(prob_ready, 1)

            def residual_bias(b):
                pool.wait_ge(xn_ready, b + 1)
                pool.wait_ge(bo_ready, 1)
                xb = x_all[:, bass.ds(b, 1), :, :].rearrange("p o t d -> p (o t) d")
                nc.gpsimd.tensor_tensor(xb, xb, bo_t[:, :].unsqueeze(1).broadcast_to([P, NT, D]),
                                        ALU.add).then_inc(xb_ready, 1)

            def xn2_low(b):
                pool.wait_ge(xn2h_ready, b + 1)
                nc.gpsimd.tensor_tensor(xn2_l[:, :, :], xn2[:, :, :], xn2_h[:, :, :].bitcast(F32),
                                        ALU.subtract).then_inc(xn2l_ready, 1)

            def first_prep(p):
                if p == 0:
                    pool.wait_ge(mu_loaded, 16)
                    nc.gpsimd.tensor_tensor(mu_sq[:, :, :], mu_raw[:, :, :], mu_raw[:, :, :], ALU.mult).then_inc(musq_ready, 1)
                if p < 4:
                    pool.wait_ge(woh_ready, p + 1)
                    c = slice(p * PAIRS // 4, (p + 1) * PAIRS // 4)
                    nc.gpsimd.tensor_tensor(wo_l[:, c, :], wo_raw[:, c, :], wo_h[:, c, :].bitcast(F32),
                                            ALU.subtract).then_inc(wol_ready, 1)
                if p == 5:
                    pool.wait_ge(murn_ready, 1)
                    nc.gpsimd.tensor_tensor(mu_sq[:, :, :], mu_raw[:, :, :],
                                            mu_nt[:, 4, :].unsqueeze(1).broadcast_to([P, DC, ES]),
                                            ALU.mult).then_inc(muunit_ready, 1)

            def step_loop(b, first, last):
                for p in range(PAIRS):
                    if not first:
                        if p == 1:
                            residual_bias(b - 1)
                        if p == 4:
                            xn2_low(b - 1)
                    normalise(b, p)
                    if first:
                        first_prep(p)

            batches(nc.gpsimd, step_loop)
            residual_bias(B - 1)
            xn2_low(B - 1)

        @block.scalar
        def _(act):
            for c in range(2):
                n = slice(c * INNER // 2, (c + 1) * INNER // 2)
                act.dma_start(wq_raw[:, :, n], rows(Wq, P)[:, :, n]).then_inc(wq_loaded[c], 16)

            def copy(dst, src, scale=1.0):
                return nc.scalar.activation(dst, src, ACT.Copy, scale=scale)

            def guess(dst, ln, a, chain, n, shift=0):
                nc.scalar.activation(ln, a, ACT.Ln, scale=float(2 ** shift)).then_inc(chain, 1)
                act.wait_ge(chain, n)
                return nc.scalar.activation(dst, ln, ACT.Exp, scale=-0.5)

            def guess1(b):
                act.wait_ge(var1_ready, b + 1)
                guess(nt1[:, 2, :], nt1[:, 1, :], nt1[:, 0, :], act_chain1, b + 1).then_inc(guess1_ready, 1)

            def xT_high(b):
                act.wait_ge(xT_done, b + 1)
                wait(act, proj_done, 8 * b)
                copy(xT_h[:, :, :].rearrange("p c n -> p (c n)"), misc_a[:, :]).then_inc(xTh_ready, 1)

            def ctxT_copy(b):
                act.wait_ge(ctxT_done, b + 1)
                wait(act, ctxT_ready, b)
                copy(ctxT_next[:, :], misc_a[:, 0:M]).then_inc(ctxT_staged, 1)

            def ctxT_move(b):
                act.wait_ge(ctxT_staged, b + 1)
                wait(act, proj_done, 8 * b)
                copy(ctxT[:, :], ctxT_next[:, :]).then_inc(ctxT_ready, 1)

            def proj_high(b, p):
                g, q, ps = 8 * b + p, p % QR, proj_ps[p % 2]
                act.wait_ge(proj_done, g + 1)
                wait(act, scores_done, g - QR + 1)
                wait(act, attn_done, g - VR + 1)
                copy(q_h[:, q, :], ps[:, 0:N], QK_SCALE)
                for h in range(2):
                    c = slice(h * HEAD, (h + 1) * HEAD)
                    copy(k_h[c, q, h * M:(h + 1) * M], ps[c, N:N + M])
                copy(v_cols(v_h, p), ps[0:M, N + M:N + M + P].rearrange("m (h d) -> m h d", h=2)).then_inc(projh_ready, 1)

            def exps(b, p):
                g, r = 8 * b + p, p % 2
                act.wait_ge(negmax_ready, g + 1)
                wait(act, probT_done, g - 1)
                wait(act, rec_ready, g - 1)
                for t in range(NT):
                    for h in range(2):
                        j = 2 * t + h
                        last = nc.scalar.activation(prob[:, r, t, h, :], scores_ps[r][:, j * M:(j + 1) * M], ACT.Exp,
                                                    bias=neg_max[:, r, j:j + 1], accum_out=prob_sum[:, r, j:j + 1])
                last.then_inc(exp_done, 1)

            def probT_high(b, p):
                g, r = 8 * b + p, p % 2
                act.wait_ge(probT_done, g + 1)
                wait(act, attn_done, g - 1)
                copy(probT_h[:, r, :], probT_ps[0:M, :]).then_inc(pth_ready, 1)

            def attn_high(b, p):
                g = 8 * b + p
                act.wait_ge(attn_done, g + 1)
                if p == 0:
                    wait(act, y_done, b)
                copy(attn_h[:, p, :], attn_ps[:, 0:N]).then_inc(attnh_ready, 1)

            def guess2(b):
                act.wait_ge(var2_ready, b + 1)
                guess(nt2[:, 2, :], nt2[:, 1, :], nt2[:, 0, :], act_chain2, b + 1).then_inc(guess2_ready, 1)

            def square_sums(b):
                act.wait_ge(xn2_ready, b + 1)
                wait(act, ssm_ready, b)
                for t in range(NT):
                    last = nc.scalar.activation(squares[:, t, :], xn2[:, t, :], ACT.Square, accum_out=nt3[:, 5, t:t + 1])
                last.then_inc(ss_ready, 1)

            def xn2_high(b):
                act.wait_ge(xn2_ready, b + 1)
                wait(act, slotin_done, b)
                copy(xn2_h[:, :, :], xn2[:, :, :]).then_inc(xn2h_ready, 1)

            def guess3(b):
                act.wait_ge(ssm_ready, b + 1)
                guess(nt3[:, 2, :], nt3[:, 1, :], nt3[:, 0, :], act_chain3, b + 1, LN_SHIFT).then_inc(guess3_ready, 1)

            def xn2T_high(b):
                act.wait_ge(xn2T_done, b + 1)
                copy(xn2T_h[:, :, :].rearrange("p c n -> p (c n)"), misc_b[:, :]).then_inc(xn2Th_ready, 1)

            def logits_scaled(b):
                act.wait_ge(logits_done, b + 1)
                act.wait_ge(rs_ready, b + 1)
                wait(act, cexp_ready, b)
                for t in range(NT):
                    last = copy(logit[:, t, :], misc_b[:, t * ES:(t + 1) * ES], nt3[:, 6, t:t + 1])
                last.then_inc(logit_ready, 1)

            def comb_exp(b):
                act.wait_ge(allmax_ready, b + 1)
                wait(act, combT_done, b)
                for t in range(NT):
                    last = nc.scalar.activation(comb[:, t, :], logit[:, t, :], ACT.Exp, bias=neg_max_all[:, t:t + 1],
                                                accum_out=comb_sum[:, t:t + 1])
                last.then_inc(cexp_ready, 1)

            def disp_exp(b):
                act.wait_ge(slotmax_ready, b + 1)
                wait(act, disp_done, b)
                for c in range(EC):
                    last = nc.scalar.activation(dispT[:, c, :], misc_b[:, c * N:(c + 1) * N], ACT.Exp,
                                                bias=neg_max_slot[:, c:c + 1], accum_out=disp_sum[:, c:c + 1])
                last.then_inc(dexp_ready, 1)

            def disp_high(b):
                act.wait_ge(disp_done, b + 1)
                wait(act, slotin_done, b)
                copy(disp_h[:, :, :].rearrange("p t e -> p (t e)"), misc_a[:, :]).then_inc(disph_ready, 1)

            def combT_high(b):
                act.wait_ge(combT_done, b + 1)
                copy(combT_h[:, bass.ds(b, 1), :, :].rearrange("p o c n -> p (o c n)"), misc_b[:, :]).then_inc(combTh_ready, 1)

            def slot_in_copy(b):
                act.wait_ge(slotin_done, b + 1)
                copy(slot_in[:, :, :, :, bass.ds(b, 1)].rearrange("p c e s o -> p (c e s o)"),
                     misc_a[:, :]).then_inc(slotin_ready, 1)

            act.wait_ge(gates_loaded, 32)
            nc.scalar.activation(tanhs[:, :], gates[:, :], ACT.Tanh).then_inc(tanh_ready, 1)
            nc.scalar.preload_act_table_set("natural_log_exp_and_others")
            guess1(0)

            def wq_high(c):
                n = slice(c * INNER // 2, (c + 1) * INNER // 2)
                act.wait_ge(wq_loaded[c], 16)
                copy(wq_h[:, :, n], wq_raw[:, :, n]).then_inc(wqh_ready, 1)

            wq_high(0)
            ctxT_copy(0)
            ctxT_move(0)
            xT_high(0)
            act.wait_ge(zeros_ready, 4)
            for p in range(AHEAD):
                proj_high(0, p)
            wq_high(1)
            exps(0, 0)

            def first_prep(p):
                if p < 4:
                    act.wait_ge(wo_loaded, 16)
                    c = slice(p * PAIRS // 4, (p + 1) * PAIRS // 4)
                    copy(wo_h[:, c, :], wo_raw[:, c, :]).then_inc(woh_ready, 1)
                if p == 3:
                    act.wait_ge(muss_ready, 1)
                    guess(mu_nt[:, 2, :], mu_nt[:, 1, :], mu_nt[:, 0, :], mu_act, 1, LN_SHIFT).then_inc(muguess_ready, 1)
                if p == 6:
                    act.wait_ge(muunit_ready, 1)
                    copy(mu_h[:, :, :], mu_sq[:, :, :]).then_inc(muh_ready, 1)

            def step_loop(b, first, last):
                for p in range(PAIRS):
                    if not first:
                        if p == 4:
                            guess3(b - 1)
                        if p == 6:
                            comb_exp(b - 1)
                    near(exps, b, p, 1, first, last)
                    if not last:
                        if p == 0:
                            ctxT_copy(b + 1)
                        if p == 4:
                            xT_high(b + 1)
                    if not first and p == 5:
                        disp_exp(b - 1)
                    near(proj_high, b, p, AHEAD, first, last)
                    if not first:
                        if p == 3:
                            square_sums(b - 1)
                            xn2T_high(b - 1)
                        if p == 4:
                            logits_scaled(b - 1)
                        if p == 6:
                            disp_high(b - 1)
                        if p == 7:
                            combT_high(b - 1)
                    probT_high(b, p)
                    if not last and p == 4:
                        ctxT_move(b + 1)
                    if not first:
                        if p == 2:
                            guess2(b - 1)
                        if p == 3:
                            xn2_high(b - 1)
                    near(attn_high, b, p, -1, first, last)
                    if not last and p == 0:
                        guess1(b + 1)
                    if not first and p == 7:
                        slot_in_copy(b - 1)
                    if first:
                        first_prep(p)

            batches(nc.scalar, step_loop)
            attn_high(B - 1, PAIRS - 1)
            guess2(B - 1)
            square_sums(B - 1)
            xn2_high(B - 1)
            guess3(B - 1)
            xn2T_high(B - 1)
            logits_scaled(B - 1)
            disp_exp(B - 1)
            comb_exp(B - 1)
            disp_high(B - 1)
            combT_high(B - 1)
            slot_in_copy(B - 1)

            act.wait_ge(b1T_done, 1)
            copy(b1T[:, :], attn_ps[0:H, 0:E]).then_inc(b1T_ready, 1)
            act.wait_ge(b1T_ready, 1)
            for k in range(E // EQ):
                act.wait_ge(hid_done, k + 1)
                for i in range(EQ):
                    e = k * EQ + i
                    last = nc.scalar.activation(hidT[0:H, e, :], scores_ps[k % 2][0:H, i * SLOTS:(i + 1) * SLOTS], ACT.Gelu,
                                                bias=b1T[:, e:e + 1])
                last.then_inc(hid_ready, 1)
            for b in range(B):
                act.wait_ge(so_back[b], 16)
                wait(act, mix_done, b - MR + 1)
                copy(so_h[:, b % MR, :, :], so_rx[:, b, :, :]).then_inc(soh_ready, 1)

        @block.vector
        def _(dve):
            V = nc.vector

            def split(dst_l, src, dst_h, scale=None):
                if scale is None:
                    return V.tensor_tensor(dst_l, src, dst_h.bitcast(F32), ALU.subtract)
                return V.scalar_tensor_tensor(dst_l, src, scale, dst_h.bitcast(F32), ALU.mult, ALU.subtract)

            def link(ins, chain, n):
                ins.then_inc(chain, 1)
                dve.wait_ge(chain, n)

            def hold():
                V.memset(pause[:, :], 0.0)

            def newton(t, chain, n):
                link(V.scalar_tensor_tensor(t[:, 3, :], t[:, 2, :], -0.5, t[:, 2, :], ALU.mult, ALU.mult), chain, n)
                link(V.tensor_tensor(t[:, 3, :], t[:, 3, :], t[:, 0, :], ALU.mult), chain, n + 1)
                return V.scalar_tensor_tensor(t[:, 4, :], t[:, 3, :], 1.5, t[:, 2, :], ALU.add, ALU.mult)

            NORM1 = 2 + 3
            FFN = 3 + 3 + 4 + 2

            def moments(tile_of, stats, mv, chain, n):
                for t in range(NT):
                    last = V.bn_stats(stats[:, t, :], tile_of(t))
                link(last, chain, n)
                hold()
                for t in range(NT):
                    last = V.bn_aggr(mv[:, t, :], stats[:, t, :])
                link(last, chain, n + 1)

            def x_tile(b, t):
                return x_all[:, bass.ds(b, 1), t, :].rearrange("p o d -> p (o d)")

            def norm1_stats(b, loaded):
                dve.wait_ge(loaded, 16)
                moments(lambda t: x_tile(b, t), stats1, mv1, norm1_chain, NORM1 * b + 1)
                V.tensor_scalar(nt1[:, 0, :], mv1[:, :, 1], 1.0, LN_EPS, ALU.mult, ALU.add).then_inc(var1_ready, 1)

            def norm1(b):
                dve.wait_ge(guess1_ready, b + 1)
                link(newton(nt1, norm1_chain, NORM1 * b + 3), norm1_chain, NORM1 * b + 5)
                wait(dve, xT_done, b)
                for t in range(NT):
                    last = V.tensor_scalar(xn[:, t, :], x_tile(b, t), mv1[:, t, 0:1], nt1[:, 4, t:t + 1],
                                           ALU.subtract, ALU.mult)
                last.then_inc(xn_ready, 1)

            def xT_low(b):
                dve.wait_ge(xTh_ready, b + 1)
                split(xT_l[:, :, :].rearrange("p c n -> p (c n)"), misc_a[:, :],
                      xT_h[:, :, :].rearrange("p c n -> p (c n)")).then_inc(xTl_ready, 1)

            def proj_low(b, p):
                g, q, ps = 8 * b + p, p % QR, proj_ps[p % 2]
                dve.wait_ge(projh_ready, g + 1)
                split(q_l[:, q, :], ps[:, 0:N], q_h[:, q, :], QK_SCALE)
                for h in range(2):
                    c = slice(h * HEAD, (h + 1) * HEAD)
                    m = slice(h * M, (h + 1) * M)
                    split(k_l[c, q, m], ps[c, N:N + M], k_h[c, q, m])
                split(v_cols(v_l, p), ps[0:M, N + M:N + M + P].rearrange("m (h d) -> m h d", h=2),
                      v_cols(v_h, p)).then_inc(projl_ready, 1)

            def maxima(b, p):
                g, r = 8 * b + p, p % 2
                dve.wait_ge(scores_done, g + 1)
                wait(dve, exp_done, g - 1)
                V.tensor_reduce(neg_max[:, r, :], scores_ps[r][:, 0:4 * M].rearrange("p (j m) -> p j m", m=M),
                                axis=AX.X, op=ALU.max, negate=True).then_inc(negmax_ready, 1)

            def probT_low(b, p):
                g, r = 8 * b + p, p % 2
                dve.wait_ge(pth_ready, g + 1)
                split(probT_l[:, r, :], probT_ps[0:M, :], probT_h[:, r, :]).then_inc(ptl_ready, 1)

            def attn_low(b, p):
                g = 8 * b + p
                dve.wait_ge(attnh_ready, g + 1)
                split(attn_l[:, p, :], attn_ps[:, 0:N], attn_h[:, p, :]).then_inc(attnl_ready, 1)

            def reciprocals(b, p):
                g, r = 8 * b + p, p % 2
                dve.wait_ge(exp_done, g + 1)
                wait(dve, prob_ready, g - 1)
                V.reciprocal(prob_rec[:, r, :], prob_sum[:, r, :]).then_inc(rec_ready, 1)

            def x1_stats(b):
                dve.wait_ge(y_done, b + 1)
                dve.wait_ge(xb_ready, b + 1)
                dve.wait_ge(tanh_ready, 1)
                for t in range(NT):
                    last = V.scalar_tensor_tensor(x_tile(b, t), (misc_a, misc_b)[t][:, 0:D], tanhs[:, 0:1], x_tile(b, t),
                                                  ALU.mult, ALU.add)
                last.then_inc(x1_ready, 1)
                dve.wait_ge(x1_ready, b + 1)
                hold()
                moments(lambda t: x_tile(b, t), stats2, mv2, ffn_chain, FFN * b + 1)
                V.tensor_scalar(nt2[:, 0, :], mv2[:, :, 1], 1.0 + LN_EPS, LN_EPS * LN_EPS, ALU.mult, ALU.add)\
                    .then_inc(var2_ready, 1)

            def x1_gamma(b):
                dve.wait_ge(small_loaded, 16 * 5)
                wait(dve, xn2l_ready, b)
                wait(dve, xn2T_done, b)
                for t in range(NT):
                    last = V.scalar_tensor_tensor(xn2[:, t, :], x_tile(b, t), mv2[:, t, 0:1], gamma[:, :],
                                                  ALU.subtract, ALU.mult)
                link(last, ffn_chain, FFN * b + 3)

            def x1_hat(b):
                dve.wait_ge(guess2_ready, b + 1)
                link(newton(nt2, ffn_chain, FFN * b + 4), ffn_chain, FFN * b + 6)
                for t in range(NT):
                    last = V.scalar_tensor_tensor(xn2[:, t, :], xn2[:, t, :], nt2[:, 4, t:t + 1], beta[:, :],
                                                  ALU.mult, ALU.add)
                last.then_inc(xn2_ready, 1)

            def guard_norm(b):
                dve.wait_ge(ss_ready, b + 1)
                V.tensor_scalar_max(nt3[:, 0, :], nt3[:, 5, :], NORM_EPS * NORM_EPS).then_inc(ssm_ready, 1)

            def token_scale(b):
                dve.wait_ge(guess3_ready, b + 1)
                n = FFN * b + 7
                link(V.tensor_scalar_mul(nt3[:, 2, :], nt3[:, 2, :], float(2 ** (LN_SHIFT // 2))), ffn_chain, n)
                link(newton(nt3, ffn_chain, n + 1), ffn_chain, n + 3)
                wait(dve, logit_ready, b)
                V.tensor_scalar(nt3[:, 6, :], nt3[:, 4, :], scale_t[:, 0:1], None, ALU.mult).then_inc(rs_ready, 1)

            def xn2T_low(b):
                dve.wait_ge(xn2Th_ready, b + 1)
                split(xn2T_l[:, :, :].rearrange("p c n -> p (c n)"), misc_b[:, :],
                      xn2T_h[:, :, :].rearrange("p c n -> p (c n)")).then_inc(xn2Tl_ready, 1)

            def comb_max(b):
                dve.wait_ge(logit_ready, b + 1)
                V.tensor_reduce(neg_max_all[:, :], logit[:, :, :], axis=AX.X, op=ALU.max,
                                negate=True).then_inc(allmax_ready, 1)

            def disp_max(b):
                dve.wait_ge(logitT_done, b + 1)
                V.tensor_reduce(neg_max_slot[:, :], misc_b[:, :].rearrange("p (c n) -> p c n", c=EC), axis=AX.X, op=ALU.max,
                                negate=True).then_inc(slotmax_ready, 1)

            def comb_norm(b):
                dve.wait_ge(cexp_ready, b + 1)
                link(V.reciprocal(comb_rec[:, :], comb_sum[:, :]), ffn_chain, FFN * b + 12)
                for t in range(NT):
                    last = V.tensor_scalar(comb[:, t, :], comb[:, t, :], comb_rec[:, t:t + 1], None, ALU.mult)
                last.then_inc(comb_ready, 1)

            def disp_norm(b):
                dve.wait_ge(dexp_ready, b + 1)
                link(V.reciprocal(disp_rec[:, :], disp_sum[:, :]), ffn_chain, FFN * b + 11)
                for c in range(EC):
                    last = V.tensor_scalar(dispT[:, c, :], dispT[:, c, :], disp_rec[:, c:c + 1], None, ALU.mult)
                last.then_inc(dispT_ready, 1)

            def disp_low(b):
                dve.wait_ge(disph_ready, b + 1)
                split(disp_l[:, :, :].rearrange("p t e -> p (t e)"), misc_a[:, :],
                      disp_h[:, :, :].rearrange("p t e -> p (t e)")).then_inc(displ_ready, 1)

            def combT_low(b):
                dve.wait_ge(combTh_ready, b + 1)
                ct = [c[:, bass.ds(b, 1), :, :].rearrange("p o c n -> p (o c n)") for c in (combT_h, combT_l)]
                split(ct[1], misc_b[:, :], ct[0]).then_inc(combTl_ready, 1)

            for t in (k_h, k_l):
                V.memset(t[:, :, :].rearrange("p r m -> p (r m)").bitcast(F32), 0.0).then_inc(zeros_ready, 1)
            norm1_stats(0, x0_loaded)
            norm1(0)

            def wq_low(c):
                n = slice(c * INNER // 2, (c + 1) * INNER // 2)
                dve.wait_ge(wqh_ready, c + 1)
                split(wq_l[:, :, n], wq_raw[:, :, n], wq_h[:, :, n]).then_inc(wql_ready, 1)

            wq_low(0)
            xT_low(0)
            for p in range(AHEAD):
                proj_low(0, p)
            for p in range(AHEAD_S):
                maxima(0, p)
            wq_low(1)
            reciprocals(0, 0)

            def first_prep(p):
                if p == 1:
                    dve.wait_ge(small_loaded, 16 * 5)
                    dve.wait_ge(tanh_ready, 1)
                    V.tensor_scalar(bo_t[:, :], bo_t[:, :], tanhs[:, 0:1], None, ALU.mult).then_inc(bo_ready, 1)
                if p == 2:
                    dve.wait_ge(munorm_done, 1)
                    V.tensor_scalar_max(mu_nt[:, 0, :], misc_b[:, 0:ES], NORM_EPS * NORM_EPS).then_inc(muss_ready, 1)
                if p == 4:
                    dve.wait_ge(muguess_ready, 1)
                    link(V.tensor_scalar_mul(mu_nt[:, 2, :], mu_nt[:, 2, :], float(2 ** (LN_SHIFT // 2))), mu_chain, 1)
                    newton(mu_nt, mu_chain, 2).then_inc(murn_ready, 1)
                if p == 7:
                    dve.wait_ge(muh_ready, 1)
                    split(mu_l[:, :, :], mu_sq[:, :, :], mu_h[:, :, :]).then_inc(mul_ready, 1)

            def step_loop(b, first, last):
                for p in range(PAIRS):
                    if not last and p == 1:
                        norm1(b + 1)
                    if not first:
                        if p == 4:
                            token_scale(b - 1)
                        if p == 6:
                            comb_norm(b - 1)
                    near(maxima, b, p, AHEAD_S, first, last)
                    if not first:
                        if p == 2:
                            x1_gamma(b - 1)
                        if p == 3:
                            guard_norm(b - 1)
                        if p == 5:
                            disp_norm(b - 1)
                    near(reciprocals, b, p, 1, first, last)
                    if not last and p == 4:
                        xT_low(b + 1)
                    near(proj_low, b, p, AHEAD, first, last)
                    if not last and p == 0:
                        norm1_stats(b + 1, x_loaded)
                    if not first and p == 2:
                        x1_hat(b - 1)
                    probT_low(b, p)
                    if not first:
                        if p == 1:
                            x1_stats(b - 1)
                        if p == 3:
                            xn2T_low(b - 1)
                        if p == 4:
                            disp_max(b - 1)
                    near(attn_low, b, p, -1, first, last)
                    if not first:
                        if p == 4:
                            comb_max(b - 1)
                        if p == 6:
                            disp_low(b - 1)
                        if p == 7:
                            combT_low(b - 1)
                    if first:
                        first_prep(p)

            batches(nc.vector, step_loop)
            attn_low(B - 1, PAIRS - 1)
            x1_stats(B - 1)
            x1_gamma(B - 1)
            x1_hat(B - 1)
            guard_norm(B - 1)
            token_scale(B - 1)
            xn2T_low(B - 1)
            comb_max(B - 1)
            disp_max(B - 1)
            disp_norm(B - 1)
            comb_norm(B - 1)
            disp_low(B - 1)
            combT_low(B - 1)

            dve.wait_ge(attn_done, B * PAIRS)
            dve.wait_ge(mul_ready, 1)
            V.memset(hidT[H:H + 1, :, :], 1.0).then_inc(ones_ready, 1)
            for j in range(E // 2):
                dve.wait_ge(so_done, j + 1)
                if j >= SR:
                    dve.wait_ge(so_sent[j % SR], 16)
                V.tensor_copy(so_tx[:, j % SR, :, :].rearrange("p e d -> p (e d)"), proj_ps[j % 2][:, :]).then_inc(so_ready, 1)

            mix_ps = (scores_ps[0], scores_ps[1], attn_ps, probT_ps)

            def mix_out(b):
                dve.wait_ge(mix_done, b + 1)
                if b >= MR:
                    dve.wait_ge(out_sent[b % MR], 16 * (b // MR))
                V.scalar_tensor_tensor(out_t[:, b % MR, :, :].rearrange("p t d -> p (t d)"), mix_ps[b % MR][:, :],
                                       tanhs[:, 1:2], x_all[:, b, :, :].rearrange("p t d -> p (t d)"),
                                       ALU.mult, ALU.add).then_inc(out_ready, 1)

            for b in range(B):
                dve.wait_ge(soh_ready, b + 1)
                split(so_l[:, b % MR, :, :], so_rx[:, b, :, :], so_h[:, b % MR, :, :]).then_inc(sol_ready, 1)
                if b > 1:
                    mix_out(b - 2)
            mix_out(B - 2)
            mix_out(B - 1)

        @block.tensor
        def _(pe):
            def product(o, terms, start=True, stop=True):
                n = 3 * len(terms)
                i = 0
                for ah, al, bh, bl in terms:
                    for lhs, rhs in ((ah, bh), (ah, bl), (al, bh)):
                        last = nc.tensor.matmul(o, lhs, rhs, start=start and i == 0, stop=stop and i == n - 1)
                        i += 1
                return last

            def xT(b):
                pe.wait_ge(xn_ready, b + 1)
                pe.wait_ge(ctxT_staged, b + 1)
                wait(pe, x1_ready, b - 1)
                for t in range(NT):
                    for c in range(DC):
                        last = nc.tensor.transpose(misc_a[:, c * N + t * P:c * N + (t + 1) * P],
                                                   xn[:, t, c * P:(c + 1) * P], ident[:, :])
                last.then_inc(xT_done, 1)

            def transpose_ctx(b):
                pe.wait_ge(ctx_loaded, 16 * (b + 1))
                wait(pe, xTl_ready, b)
                wait(pe, slotin_ready, b - 2)
                nc.tensor.transpose(misc_a[:, 0:M], ctx_in[:, :], ident[0:M, 0:M]).then_inc(ctxT_done, 1)

            def project(b, p):
                g, ps = 8 * b + p, proj_ps[p % 2]
                if p == 0:
                    pe.wait_ge(xTl_ready, b + 1)
                    pe.wait_ge(ctxT_ready, b + 1)
                wait(pe, projl_ready, g - 1)
                c = slice(p * P, (p + 1) * P)
                product(ps[:, 0:N], [(wq_h[:, k, c], wq_l[:, k, c], xT_h[:, k, :], xT_l[:, k, :]) for k in range(DC)])
                nc.tensor.matmul(ps[:, N:N + M], wk[:, c], ctxT[:, :], start=True, stop=True)
                nc.tensor.matmul(ps[0:M, N + M:N + M + P], ctxT[:, :], wv[:, c], start=True, stop=True)\
                    .then_inc(proj_done, 1)

            def score(b, p):
                g, r, q = 8 * b + p, p % 2, p % QR
                pe.wait_ge(projl_ready, g + 1)
                wait(pe, exp_done, g - 1)
                for t in range(NT):
                    c = slice(t * P, (t + 1) * P)
                    last = product(scores_ps[r][:, t * K2:(t + 1) * K2],
                                   [(q_h[:, q, c], q_l[:, q, c], k_h[:, q, :], k_l[:, q, :])])
                last.then_inc(scores_done, 1)

            def transpose_prob(b, p):
                g, r = 8 * b + p, p % 2
                pe.wait_ge(prob_ready, g + 1)
                wait(pe, ptl_ready, g)
                for h in range(2):
                    for t in range(NT):
                        o = h * N + t * P
                        last = nc.tensor.transpose(probT_ps[0:M, o:o + P], prob[:, r, t, h, :], ident[:, :])
                last.then_inc(probT_done, 1)

            def attend(b, p):
                g, r, v = 8 * b + p, p % 2, p % VR
                pe.wait_ge(ptl_ready, g + 1)
                wait(pe, attnl_ready, g)
                product(attn_ps[:, 0:N], [(v_h[:, v, h, :], v_l[:, v, h, :], probT_h[:, r, h * N:(h + 1) * N],
                                           probT_l[:, r, h * N:(h + 1) * N]) for h in range(2)]).then_inc(attn_done, 1)

            def output_projection(b, half, context_between):
                if half == 0:
                    pe.wait_ge(wol_ready, 4)
                    wait(pe, combTl_ready, b)
                    if context_between:
                        pe.wait_ge(ctxT_staged, b + 3)
                    else:
                        pe.wait_ge(slotin_ready, b)
                else:
                    pe.wait_ge(attnl_ready, 8 * b + 8)
                for t in range(NT):
                    c = slice(t * P, (t + 1) * P)
                    last = product((misc_a, misc_b)[t][:, 0:D],
                                   [(attn_h[:, k, c], attn_l[:, k, c], wo_h[:, k, :], wo_l[:, k, :])
                                    for k in range(half * PAIRS // 2, (half + 1) * PAIRS // 2)],
                                   start=half == 0, stop=half == 1)
                if half == 1:
                    last.then_inc(y_done, 1)

            def transpose_xn2(b):
                pe.wait_ge(xn2_ready, b + 1)
                for t in range(NT):
                    for c in range(DC):
                        last = nc.tensor.transpose(misc_b[:, c * N + t * P:c * N + (t + 1) * P],
                                                   xn2[:, t, c * P:(c + 1) * P], ident[:, :])
                last.then_inc(xn2T_done, 1)

            def logits(b):
                pe.wait_ge(xn2Tl_ready, b + 1)
                pe.wait_ge(mul_ready, 1)
                for t in range(NT):
                    c = slice(t * P, (t + 1) * P)
                    last = product(misc_b[:, t * ES:(t + 1) * ES],
                                   [(xn2T_h[:, k, c], xn2T_l[:, k, c], mu_h[:, k, :], mu_l[:, k, :]) for k in range(DC)])
                last.then_inc(logits_done, 1)

            def transpose_logits(b):
                pe.wait_ge(logit_ready, b + 1)
                for c in range(EC):
                    for t in range(NT):
                        last = nc.tensor.transpose(misc_b[:, c * N + t * P:c * N + (t + 1) * P],
                                                   logit[:, t, c * P:(c + 1) * P], ident[:, :])
                last.then_inc(logitT_done, 1)

            def transpose_disp(b):
                pe.wait_ge(dispT_ready, b + 1)
                for t in range(NT):
                    for c in range(EC):
                        last = nc.tensor.transpose(misc_a[:, t * ES + c * P:t * ES + (c + 1) * P],
                                                   dispT[:, c, t * P:(t + 1) * P], ident[:, :])
                last.then_inc(disp_done, 1)

            def transpose_comb(b):
                pe.wait_ge(comb_ready, b + 1)
                for c in range(EC):
                    for t in range(NT):
                        last = nc.tensor.transpose(misc_b[:, c * N + t * P:c * N + (t + 1) * P],
                                                   comb[:, t, c * P:(c + 1) * P], ident[:, :])
                last.then_inc(combT_done, 1)

            def slot_inputs(b):
                pe.wait_ge(displ_ready, b + 1)
                pe.wait_ge(xn2l_ready, b + 1)
                for c in range(DC):
                    d = slice(c * P, (c + 1) * P)
                    last = product(misc_a[:, c * ES:(c + 1) * ES],
                                   [(xn2_h[:, t, d], xn2_l[:, t, d], disp_h[:, t, :], disp_l[:, t, :]) for t in range(NT)])
                last.then_inc(slotin_done, 1)

            pe.wait_ge(ident_ready, 1)
            transpose_ctx(0)
            xT(0)
            pe.wait_ge(wkv_loaded, 32)
            pe.wait_ge(wql_ready, 1)
            for p in range(AHEAD):
                project(0, p)
            for p in range(AHEAD_S):
                score(0, p)

            def step_loop(b, first, last):
                for p in range(PAIRS):
                    if first and p == PAIRS // 2 - AHEAD:
                        pe.wait_ge(wql_ready, 2)
                    if not first:
                        if p == 1:
                            output_projection(b - 1, 0, not last)
                        if p == 5:
                            transpose_logits(b - 1)
                        if p == 7:
                            transpose_comb(b - 1)
                    near(project, b, p, AHEAD, first, last)
                    if not first and p == 6:
                        transpose_disp(b - 1)
                    near(score, b, p, AHEAD_S, first, last)
                    if not last and p == 0:
                        transpose_ctx(b + 1)
                    if not last and p == 3:
                        xT(b + 1)
                    if not first:
                        if p == 3:
                            transpose_xn2(b - 1)
                        if p == 4:
                            logits(b - 1)
                    transpose_prob(b, p)
                    if not first and p == 1:
                        output_projection(b - 1, 1, not last)
                    near(attend, b, p, -1, first, last)
                    if not first and p == 7:
                        slot_inputs(b - 1)
                    if first and p == 1:
                        pe.wait_ge(musq_ready, 1)
                        for c in range(DC):
                            mm = nc.tensor.matmul(misc_b[:, 0:ES], ones[:, :], mu_sq[:, c, :],
                                                  start=c == 0, stop=c == DC - 1)
                        mm.then_inc(munorm_done, 1)
                    if first and p == 7:
                        pe.wait_ge(muss_ready, 1)

            batches(nc.tensor, step_loop)
            output_projection(B - 1, 0, False)
            attend(B - 1, PAIRS - 1)
            output_projection(B - 1, 1, False)
            transpose_xn2(B - 1)
            logits(B - 1)
            transpose_logits(B - 1)
            transpose_disp(B - 1)
            transpose_comb(B - 1)
            slot_inputs(B - 1)

            pe.wait_ge(small_loaded, 16 * 5)
            pe.wait_ge(attnl_ready, 8 * B)
            nc.tensor.transpose(attn_ps[0:H, 0:E], b1_in[:, :], ident[0:E, 0:E]).then_inc(b1T_done, 1)

            pe.wait_ge(exp_loaded, 48)
            pe.wait_ge(slotin_ready, B)
            for k in range(E // EQ):
                if k >= 2:
                    pe.wait_ge(hid_ready, k - 1)
                for i in range(EQ):
                    e = k * EQ + i
                    for c in range(DC):
                        last = nc.tensor.matmul(scores_ps[k % 2][0:H, i * SLOTS:(i + 1) * SLOTS], w1_t[:, e, c, :],
                                                slot_in[:, c, e, :, :].rearrange("p s b -> p (s b)"),
                                                start=c == 0, stop=c == DC - 1)
                last.then_inc(hid_done, 1)
            pe.wait_ge(ones_ready, 1)
            for j in range(E // 2):
                pe.wait_ge(hid_ready, 2 * j // EQ + 1)
                if j >= 2:
                    pe.wait_ge(so_ready, j - 1)
                for i in range(2):
                    last = nc.tensor.matmul(proj_ps[j % 2][:, i * D:(i + 1) * D], hidT[:, 2 * j + i, :],
                                            w2_t[:, 2 * j + i, :], start=True, stop=True)
                last.then_inc(so_done, 1)
            mix_ps = (scores_ps[0], scores_ps[1], attn_ps, probT_ps)
            for b in range(B):
                pe.wait_ge(sol_ready, b + 1)
                if b == 2:
                    pe.wait_ge(b1T_ready, 1)
                if b >= MR:
                    pe.wait_ge(out_ready, b - MR + 1)
                for t in range(NT):
                    c = slice(t * P, (t + 1) * P)
                    last = product(mix_ps[b % MR][:, t * D:(t + 1) * D],
                                   [(combT_h[:, b, k, c], combT_l[:, b, k, c], so_h[:, b % MR, k, :], so_l[:, b % MR, k, :])
                                    for k in range(EC)])
                last.then_inc(mix_done, 1)


_INS = ['x', 'ctx_512', 'g_xattn', 'g_ffn', 'L0_xattn_Wq', 'L0_xattn_Wk', 'L0_xattn_Wv', 'L0_xattn_Wo', 'L0_xattn_bo',
        'L0_ffn_ln_gamma', 'L0_ffn_ln_beta', 'L0_ffn_mu', 'L0_ffn_scale', 'L0_ffn_w1', 'L0_ffn_b1', 'L0_ffn_w2', 'L0_ffn_b2']


def kernel(**inputs):
    import concourse.bacc as _bacc
    from concourse.bass_utils import run_bass_kernel_spmd as _run

    nc = _bacc.Bacc("TRN2", target_bir_lowering=False, num_devices=1)
    arrays, args = {}, []
    for name in _INS:
        a = np.ascontiguousarray(inputs[name])
        arrays[f"in_{name}_dram"] = a
        args.append(nc.dram_tensor(f"in_{name}_dram", a.shape, mybir.dt.from_np(a.dtype), kind="ExternalInput").ap())
    shape = inputs['x'].shape
    args.append(nc.dram_tensor("out_0_dram", shape, F32, kind="ExternalOutput").ap())
    flamingo_layer(nc, *args)
    r = _run(nc, [arrays], core_ids=[0])
    return r.results[0]["out_0_dram"]
```

```python
from contextlib import ExitStack

import numpy as np
import concourse.bass as bass
from concourse import mybir

F32 = mybir.dt.float32
F32R = mybir.dt.float32r
ALU = mybir.AluOpType
ACT = mybir.ActivationFunctionType
AX = mybir.AxisListType

P = 128
HEAD = 64
LN_EPS = 1e-5
NORM_EPS = 1e-12
LN_SHIFT = 20



def rows(ap, p):
    return ap.rearrange("(t p) d -> p t d", p=p)


def flamingo_layer(nc, x, ctx_kv, g_xattn, g_ffn, Wq, Wk, Wv, Wo, bo, ln_gamma, ln_beta, mu, scale,
                   w1, b1, w2, b2, out):
    B, N, D = x.shape
    M, KV = ctx_kv.shape[1:]
    INNER = Wq.shape[1]
    PAIRS = INNER // P
    NT = N // P
    DC = D // P
    _, E, S = mu.shape
    ES = E * S
    EC = ES // P
    H = w1.shape[2]
    assert KV == P and D == 2 * P and N == 2 * P and ES == 2 * P and PAIRS % 4 == 0 and 4 * M <= 512
    K2 = 2 * M
    QK_SCALE = float(HEAD) ** -0.5
    EQ = 4
    AHEAD = 3
    AHEAD_S = AHEAD - 1
    QR = 4
    VR = 8
    MR = 4

    with ExitStack() as top:
        def sb(stack, name, shape, dt=F32):
            return stack.enter_context(nc.sbuf_tensor(name, shape, dt))

        def sem(name):
            return top.enter_context(nc.semaphore(name))

        def bank(name):
            return top.enter_context(nc.psum_tensor(name, [P, 512], F32))

        scores_ps = [bank(f"scores_ps{i}") for i in range(2)]
        proj_ps = [bank(f"proj_ps{i}") for i in range(2)]
        probT_ps = bank("probT_ps")
        attn_ps = bank("attn_ps")
        misc_a = bank("misc_a")
        misc_b = bank("misc_b")

        y_last_ps = proj_ps
        hid_ps = (scores_ps[0], scores_ps[1], probT_ps, attn_ps)
        so_ps = (proj_ps[0], proj_ps[1], scores_ps[0], scores_ps[1])
        back_ps = (probT_ps, attn_ps)
        mix_ps = scores_ps

        x_all = sb(top, "x_all", [P, B, NT, D])
        wo_h = sb(top, "wo_h", [P, PAIRS, D], F32R)
        wo_l = sb(top, "wo_l", [P, PAIRS, D], F32R)
        mu_h = sb(top, "mu_h", [P, DC, ES], F32R)
        mu_l = sb(top, "mu_l", [P, DC, ES], F32R)
        combT_h = sb(top, "combT_h", [P, B, EC, N], F32R)
        combT_l = sb(top, "combT_l", [P, B, EC, N], F32R)
        slot_in = sb(top, "slot_in", [P, DC, B, E, S])
        attn_h = sb(top, "attn_h", [P, PAIRS, N], F32R)
        attn_l = sb(top, "attn_l", [P, PAIRS, N], F32R)
        xn2 = sb(top, "xn2", [P, NT, D])
        xn2_h = sb(top, "xn2_h", [P, NT, D], F32R)
        xn2_l = sb(top, "xn2_l", [P, NT, D], F32R)
        xn2T_h = sb(top, "xn2T_h", [P, DC, N], F32R)
        xn2T_l = sb(top, "xn2T_l", [P, DC, N], F32R)
        logit = sb(top, "logit", [P, NT, ES])
        dispT = sb(top, "dispT", [P, EC, N])
        disp_h = sb(top, "disp_h", [P, NT, ES], F32R)
        disp_l = sb(top, "disp_l", [P, NT, ES], F32R)
        comb = sb(top, "comb", [P, NT, ES])
        squares = sb(top, "squares", [P, NT, D])
        gamma = sb(top, "gamma", [P, D])
        beta = sb(top, "beta", [P, D])
        bo_t = sb(top, "bo_t", [P, D])
        ident = sb(top, "ident", [P, P])
        b1_in = sb(top, "b1_in", [E, H])
        b1T = sb(top, "b1T", [H, E])
        gates = sb(top, "gates", [P, 2])
        tanhs = sb(top, "tanhs", [P, 2])
        scale_t = sb(top, "scale_t", [P, 1])
        pause = sb(top, "pause", [P, 1])
        stats1 = sb(top, "stats1", [P, NT, 6])
        mv1 = sb(top, "mv1", [P, NT, 2])
        nt1 = sb(top, "nt1", [P, 5, NT])
        stats2 = sb(top, "stats2", [P, NT, 6])
        mv2 = sb(top, "mv2", [P, NT, 2])
        nt2 = sb(top, "nt2", [P, 5, NT])
        nt3 = sb(top, "nt3", [P, 7, NT])
        neg_max_slot = sb(top, "neg_max_slot", [P, EC])
        neg_max_all = sb(top, "neg_max_all", [P, NT])
        disp_sum = sb(top, "disp_sum", [P, EC])
        disp_rec = sb(top, "disp_rec", [P, EC])
        comb_sum = sb(top, "comb_sum", [P, NT])
        comb_rec = sb(top, "comb_rec", [P, NT])
        wq_raw = slot_in[:, :, :, :, :].rearrange("p c b e s -> p (c b e s)")[:, 0:DC * INNER]\
            .rearrange("p (c n) -> p c n", c=DC)
        wo_raw = slot_in[:, :, :, :, :].rearrange("p c b e s -> p (c b e s)")[:, DC * INNER:DC * INNER + PAIRS * D]\
            .rearrange("p (c n) -> p c n", c=PAIRS)

        with ExitStack() as attention:
            wq_h = sb(attention, "wq_h", [P, DC, INNER], F32R)
            wq_l = sb(attention, "wq_l", [P, DC, INNER], F32R)
            wk = sb(attention, "wk", [P, INNER])
            wv = sb(attention, "wv", [P, INNER])
            ctx_in = sb(attention, "ctx_in", [M, KV])
            ctxT = sb(attention, "ctxT", [P, M])
            ctxT_next = sb(attention, "ctxT_next", [P, M])
            xn = sb(attention, "xn", [P, NT, D])
            xT_h = sb(attention, "xT_h", [P, DC, N], F32R)
            xT_l = sb(attention, "xT_l", [P, DC, N], F32R)
            q_h = sb(attention, "q_h", [P, QR, N], F32R)
            q_l = sb(attention, "q_l", [P, QR, N], F32R)
            k_h = sb(attention, "k_h", [P, QR, K2], F32R)
            k_l = sb(attention, "k_l", [P, QR, K2], F32R)
            v_h = sb(attention, "v_h", [M, VR, 2, P], F32R)
            v_l = sb(attention, "v_l", [M, VR, 2, P], F32R)
            prob = sb(attention, "prob", [P, 2, NT, 2, M])
            probT_h = sb(attention, "probT_h", [M, 2, 2 * N], F32R)
            probT_l = sb(attention, "probT_l", [M, 2, 2 * N], F32R)
            neg_max = sb(attention, "neg_max", [P, 2, NT * 2])
            prob_sum = sb(attention, "prob_sum", [P, 2, NT * 2])
            prob_rec = sb(attention, "prob_rec", [P, 2, NT * 2])
            mu_raw, mu_sq = comb, logit
            mu_nt = sb(attention, "mu_nt", [P, 5, ES])
            ones = sb(attention, "ones", [P, P])

        with ExitStack() as experts:
            w1_t = sb(experts, "w1_t", [P, E, DC, H])
            w2_t = sb(experts, "w2_t", [H + 1, E, D])
            hidT = sb(experts, "hidT", [H + 1, E, S, B])
            soT = sb(experts, "soT", [P, DC, E, S, B])
            so_h = sb(experts, "so_h", [P, MR, EC, D], F32R)
            so_l = sb(experts, "so_l", [P, MR, EC, D], F32R)
            out_t = sb(experts, "out_t", [P, MR, NT, D])

        x0_loaded, x_loaded, ctx_loaded = sem("x0_loaded"), sem("x_loaded"), sem("ctx_loaded")
        wq_loaded, wkv_loaded, wo_loaded = [sem(f"wq_loaded{i}") for i in range(2)], sem("wkv_loaded"), sem("wo_loaded")
        gates_loaded, small_loaded, mu_loaded, exp_loaded = sem("gates_loaded"), sem("small_loaded"), sem("mu_loaded"), sem("exp_loaded")
        consts, zeros_ready, ident_ready, tanh_ready, bo_ready = sem("consts"), sem("zeros_ready"), sem("ident_ready"), sem("tanh_ready"), sem("bo_ready")
        wqh_ready, wql_ready, wql_half_ready = sem("wqh_ready"), sem("wql_ready"), sem("wql_half_ready")
        woh_ready, wol_ready = sem("woh_ready"), sem("wol_ready")
        musq_ready, munorm_done, muss_ready = sem("musq_ready"), sem("munorm_done"), sem("muss_ready")
        muguess_ready, murn_ready, muunit_ready = sem("muguess_ready"), sem("murn_ready"), sem("muunit_ready")
        b1T_done, b1T_ready = sem("b1T_done"), sem("b1T_ready")
        muh_ready, mul_ready, mu_chain, mu_act = sem("muh_ready"), sem("mul_ready"), sem("mu_chain"), sem("mu_act")
        var1_ready, guess1_ready, xn_ready = sem("var1_ready"), sem("guess1_ready"), sem("xn_ready")
        xT_done, xTh_ready, xTl_ready = sem("xT_done"), sem("xTh_ready"), sem("xTl_ready")
        ctxT_done, ctxT_staged, ctxT_ready = sem("ctxT_done"), sem("ctxT_staged"), sem("ctxT_ready")
        norm1_chain, act_chain1 = sem("norm1_chain"), sem("act_chain1")
        proj_done, projh_ready, projl_ready = sem("proj_done"), sem("projh_ready"), sem("projl_ready")
        scores_done, negmax_ready, exp_done = sem("scores_done"), sem("negmax_ready"), sem("exp_done")
        rec_ready, prob_ready, probT_done = sem("rec_ready"), sem("prob_ready"), sem("probT_done")
        pth_ready, ptl_ready = sem("pth_ready"), sem("ptl_ready")
        attn_done, attnh_ready, attnl_ready = sem("attn_done"), sem("attnh_ready"), sem("attnl_ready")
        xb_ready, y_done, x1_ready = sem("xb_ready"), sem("y_done"), sem("x1_ready")
        var2_ready, guess2_ready, xn2_ready = sem("var2_ready"), sem("guess2_ready"), sem("xn2_ready")
        ss_ready, ssm_ready, guess3_ready, rs_ready = sem("ss_ready"), sem("ssm_ready"), sem("guess3_ready"), sem("rs_ready")
        xn2h_ready, xn2l_ready = sem("xn2h_ready"), sem("xn2l_ready")
        xn2T_done, xn2Th_ready, xn2Tl_ready = sem("xn2T_done"), sem("xn2Th_ready"), sem("xn2Tl_ready")
        logits_done, logit_ready = sem("logits_done"), sem("logit_ready")
        logitT_done, slotmax_ready, allmax_ready = sem("logitT_done"), sem("slotmax_ready"), sem("allmax_ready")
        dexp_ready, cexp_ready, dispT_ready, disp_done = sem("dexp_ready"), sem("cexp_ready"), sem("dispT_ready"), sem("disp_done")
        disph_ready, displ_ready = sem("disph_ready"), sem("displ_ready")
        comb_ready, combT_done, combTh_ready, combTl_ready = (
            sem("comb_ready"), sem("combT_done"), sem("combTh_ready"), sem("combTl_ready"))
        slotin_done, slotin_ready = sem("slotin_done"), sem("slotin_ready")
        ffn_chain, act_chain2, act_chain3 = sem("ffn_chain"), sem("act_chain2"), sem("act_chain3")
        ones_ready, hid_done, hid_ready = sem("ones_ready"), sem("hid_done"), sem("hid_ready")
        so_done, so_ready, so_back = sem("so_done"), sem("so_ready"), sem("so_back")
        soh_ready, sol_ready, mix_done, out_ready = sem("soh_ready"), sem("sol_ready"), sem("mix_done"), sem("out_ready")
        out_sent = [sem(f"out_sent{i}") for i in range(MR)]

        def wait(eng, s, n):
            if isinstance(n, int) and n <= 0:
                return
            eng.wait_ge(s, n)

        def near(stage, b, p, lag, first, last):
            if p + lag >= PAIRS:
                if not last:
                    stage(b + 1, p + lag - PAIRS)
            elif p + lag < 0:
                if not first:
                    stage(b - 1, p + lag + PAIRS)
            else:
                stage(b, p + lag)

        def v_cols(v, p):
            blocks = v[:, p % VR, :, :].rearrange("m h (k d) -> m (h k) d", d=HEAD)
            return blocks[:, 0:4:3, :]

        def batches(nc_eng, body):
            body(0, True, False)
            body(1, False, False)
            with nc_eng.Fori(2, B - 1) as b:
                body(b, False, False)
            body(B - 1, False, True)

        block = top.enter_context(nc.Block())

        @block.sync
        def _(sp):
            sp.dma_start(x_all[:, 0, :, :], rows(x[0, :, :], P)).then_inc(x0_loaded, 16)
            sp.dma_start(ctx_in[:, :], ctx_kv[0, :, :]).then_inc(ctx_loaded, 16)
            sp.dma_start(gates[:, 0:1], g_xattn.partition_broadcast(P)).then_inc(gates_loaded, 16)
            sp.dma_start(gates[:, 1:2], g_ffn.partition_broadcast(P)).then_inc(gates_loaded, 16)
            sp.dma_start(wk[:, :], Wk).then_inc(wkv_loaded, 16)
            sp.dma_start(wv[:, :], Wv).then_inc(wkv_loaded, 16)
            half = slice(INNER // 2, INNER)
            sp.dma_start(wq_raw[:, :, half], rows(Wq, P)[:, :, half]).then_inc(wq_loaded[1], 16)
            sp.dma_start(x_all[:, 1:B, :, :], x[1:B, :, :].rearrange("b (t p) d -> p b t d", p=P)).then_inc(x_loaded, 16)
            sp.dma_start(wo_raw, rows(Wo, P)).then_inc(wo_loaded, 16)
            sp.dma_start(mu_raw[:, :, :], mu.rearrange("(c p) e s -> p c (e s)", p=P)).then_inc(mu_loaded, 16)
            with nc.sync.Fori(1, B) as b:
                sp.wait_ge(ctxT_done, b)
                sp.dma_start(ctx_in[:, :], ctx_kv[bass.ds(b, 1), :, :].rearrange("o m k -> (o m) k")).then_inc(ctx_loaded, 16)
            sp.wait_ge(proj_done, B * PAIRS)
            sp.dma_start(w1_t[:, :, :, :], w1.rearrange("e (c p) h -> p e c h", p=P)).then_inc(exp_loaded, 16)
            sp.dma_start(w2_t[0:H, :, :], w2.rearrange("e h d -> h e d")).then_inc(exp_loaded, 16)
            sp.dma_start(w2_t[H:H + 1, :, :], b2.rearrange("(o e) d -> o e d", o=1)).then_inc(exp_loaded, 16)
            for b in range(B):
                sp.wait_ge(out_ready, b + 1)
                sp.dma_start(rows(out[b, :, :], P), out_t[:, b % MR, :, :]).then_inc(out_sent[b % MR], 16)
            for s in out_sent:
                sp.wait_ge(s, 16 * (B // MR))

        @block.gpsimd
        def _(pool):
            nc.gpsimd.memset(ident[:, :], 0.0).then_inc(consts, 1)
            nc.gpsimd.memset(ones[:, :], 1.0).then_inc(consts, 1)
            pool.wait_ge(consts, 2)
            pool.affine_select(out=ident[:, :], in_=ident[:, :], compare_op=ALU.not_equal, fill=1.0,
                               base=0, pattern=[[-1, P]], channel_multiplier=1).then_inc(ident_ready, 1)
            for t in (v_h, v_l):
                nc.gpsimd.memset(t[:, :, :, :].rearrange("p r h m -> p (r h m)").bitcast(F32), 0.0).then_inc(zeros_ready, 1)
            pool.dma_start(bo_t[:, :], bo.partition_broadcast(P)).then_inc(small_loaded, 16)
            pool.dma_start(scale_t[:, :], scale.partition_broadcast(P)).then_inc(small_loaded, 16)
            pool.dma_start(gamma[:, :], ln_gamma.partition_broadcast(P)).then_inc(small_loaded, 16)
            pool.dma_start(beta[:, :], ln_beta.partition_broadcast(P)).then_inc(small_loaded, 16)
            pool.dma_start(b1_in[:, :], b1).then_inc(small_loaded, 16)

            half = slice(INNER // 2, INNER)
            pool.wait_ge(wqh_ready, 2)
            nc.gpsimd.tensor_tensor(wq_l[:, :, half], wq_raw[:, :, half], wq_h[:, :, half].bitcast(F32),
                                    ALU.subtract).then_inc(wql_half_ready, 1)

            def normalise(b, p):
                g = 8 * b + p
                r = p % 2
                pool.wait_ge(exp_done, g + 1)
                pool.wait_ge(rec_ready, g + 1)
                pr = prob[:, r, :, :, :].rearrange("p t h m -> p (t h) m")
                nc.gpsimd.tensor_tensor(pr, pr, prob_rec[:, r, :].unsqueeze(2).broadcast_to([P, NT * 2, M]),
                                        ALU.mult).then_inc(prob_ready, 1)

            def residual_bias(b):
                pool.wait_ge(xn_ready, b + 1)
                pool.wait_ge(bo_ready, 1)
                xb = x_all[:, bass.ds(b, 1), :, :].rearrange("p o t d -> p (o t) d")
                nc.gpsimd.tensor_tensor(xb, xb, bo_t[:, :].unsqueeze(1).broadcast_to([P, NT, D]),
                                        ALU.add).then_inc(xb_ready, 1)

            def xn2_low(b):
                pool.wait_ge(xn2h_ready, b + 1)
                nc.gpsimd.tensor_tensor(xn2_l[:, :, :], xn2[:, :, :], xn2_h[:, :, :].bitcast(F32),
                                        ALU.subtract).then_inc(xn2l_ready, 1)

            def first_prep(p):
                if p == 0:
                    pool.wait_ge(mu_loaded, 16)
                    nc.gpsimd.tensor_tensor(mu_sq[:, :, :], mu_raw[:, :, :], mu_raw[:, :, :], ALU.mult).then_inc(musq_ready, 1)
                if 1 <= p < 5:
                    pool.wait_ge(woh_ready, p)
                    c = slice((p - 1) * PAIRS // 4, p * PAIRS // 4)
                    nc.gpsimd.tensor_tensor(wo_l[:, c, :], wo_raw[:, c, :], wo_h[:, c, :].bitcast(F32),
                                            ALU.subtract).then_inc(wol_ready, 1)
                if p == 6:
                    pool.wait_ge(murn_ready, 1)
                    nc.gpsimd.tensor_tensor(mu_sq[:, :, :], mu_raw[:, :, :],
                                            mu_nt[:, 4, :].unsqueeze(1).broadcast_to([P, DC, ES]),
                                            ALU.mult).then_inc(muunit_ready, 1)

            def step_loop(b, first, last):
                for p in range(PAIRS):
                    if not first:
                        if p == 1:
                            residual_bias(b - 1)
                        if p == 4:
                            xn2_low(b - 1)
                    normalise(b, p)
                    if first:
                        first_prep(p)

            batches(nc.gpsimd, step_loop)
            residual_bias(B - 1)
            pool.wait_ge(attn_done, B * PAIRS)
            pool.wait_ge(mul_ready, 1)
            pool.wait_ge(xb_ready, B)
            nc.gpsimd.memset(hidT[H:H + 1, :, :, :], 1.0).then_inc(ones_ready, 1)
            pool.wait_ge(ones_ready, 1)
            xn2_low(B - 1)

        @block.scalar
        def _(act):
            half = slice(0, INNER // 2)
            act.dma_start(wq_raw[:, :, half], rows(Wq, P)[:, :, half]).then_inc(wq_loaded[0], 16)

            def copy(dst, src, scale=1.0):
                return nc.scalar.activation(dst, src, ACT.Copy, scale=scale)

            def guess(dst, ln, a, chain, n, shift=0):
                nc.scalar.activation(ln, a, ACT.Ln, scale=float(2 ** shift)).then_inc(chain, 1)
                act.wait_ge(chain, n)
                return nc.scalar.activation(dst, ln, ACT.Exp, scale=-0.5)

            def guess1(b):
                act.wait_ge(var1_ready, b + 1)
                guess(nt1[:, 2, :], nt1[:, 1, :], nt1[:, 0, :], act_chain1, b + 1).then_inc(guess1_ready, 1)

            def xT_high(b):
                act.wait_ge(xT_done, b + 1)
                wait(act, proj_done, 8 * b)
                copy(xT_h[:, :, :].rearrange("p c n -> p (c n)"), misc_a[:, :]).then_inc(xTh_ready, 1)

            def ctxT_copy(b):
                act.wait_ge(ctxT_done, b + 1)
                wait(act, ctxT_ready, b)
                copy(ctxT_next[:, :], misc_a[:, 0:M]).then_inc(ctxT_staged, 1)

            def ctxT_move(b):
                act.wait_ge(ctxT_staged, b + 1)
                wait(act, proj_done, 8 * b)
                copy(ctxT[:, :], ctxT_next[:, :]).then_inc(ctxT_ready, 1)

            def proj_high(b, p):
                g, q, ps = 8 * b + p, p % QR, proj_ps[p % 2]
                act.wait_ge(proj_done, g + 1)
                wait(act, scores_done, g - QR + 1)
                wait(act, attn_done, g - VR + 1)
                copy(q_h[:, q, :], ps[:, 0:N], QK_SCALE)
                for h in range(2):
                    c = slice(h * HEAD, (h + 1) * HEAD)
                    copy(k_h[c, q, h * M:(h + 1) * M], ps[c, N:N + M])
                copy(v_cols(v_h, p), ps[0:M, N + M:N + M + P].rearrange("m (h d) -> m h d", h=2)).then_inc(projh_ready, 1)

            def exps(b, p):
                g, r = 8 * b + p, p % 2
                act.wait_ge(negmax_ready, g + 1)
                wait(act, probT_done, g - 1)
                wait(act, rec_ready, g - 1)
                for t in range(NT):
                    for h in range(2):
                        j = 2 * t + h
                        last = nc.scalar.activation(prob[:, r, t, h, :], scores_ps[r][:, j * M:(j + 1) * M], ACT.Exp,
                                                    bias=neg_max[:, r, j:j + 1], accum_out=prob_sum[:, r, j:j + 1])
                last.then_inc(exp_done, 1)

            def probT_high(b, p):
                g, r = 8 * b + p, p % 2
                act.wait_ge(probT_done, g + 1)
                wait(act, attn_done, g - 1)
                copy(probT_h[:, r, :], probT_ps[0:M, :]).then_inc(pth_ready, 1)

            def attn_high(b, p):
                g = 8 * b + p
                act.wait_ge(attn_done, g + 1)
                if p == 0:
                    wait(act, y_done, b)
                copy(attn_h[:, p, :], attn_ps[:, 0:N]).then_inc(attnh_ready, 1)

            def guess2(b):
                act.wait_ge(var2_ready, b + 1)
                guess(nt2[:, 2, :], nt2[:, 1, :], nt2[:, 0, :], act_chain2, b + 1).then_inc(guess2_ready, 1)

            def square_sums(b):
                act.wait_ge(xn2_ready, b + 1)
                wait(act, ssm_ready, b)
                for t in range(NT):
                    last = nc.scalar.activation(squares[:, t, :], xn2[:, t, :], ACT.Square, accum_out=nt3[:, 5, t:t + 1])
                last.then_inc(ss_ready, 1)

            def xn2_high(b):
                act.wait_ge(xn2_ready, b + 1)
                wait(act, slotin_done, b)
                copy(xn2_h[:, :, :], xn2[:, :, :]).then_inc(xn2h_ready, 1)

            def guess3(b):
                act.wait_ge(ssm_ready, b + 1)
                guess(nt3[:, 2, :], nt3[:, 1, :], nt3[:, 0, :], act_chain3, b + 1, LN_SHIFT).then_inc(guess3_ready, 1)

            def xn2T_high(b):
                act.wait_ge(xn2T_done, b + 1)
                copy(xn2T_h[:, :, :].rearrange("p c n -> p (c n)"), misc_b[:, :]).then_inc(xn2Th_ready, 1)

            def logits_scaled(b):
                act.wait_ge(logits_done, b + 1)
                act.wait_ge(rs_ready, b + 1)
                wait(act, cexp_ready, b)
                for t in range(NT):
                    last = copy(logit[:, t, :], misc_b[:, t * ES:(t + 1) * ES], nt3[:, 6, t:t + 1])
                last.then_inc(logit_ready, 1)

            def comb_exp(b):
                act.wait_ge(allmax_ready, b + 1)
                wait(act, combT_done, b)
                for t in range(NT):
                    last = nc.scalar.activation(comb[:, t, :], logit[:, t, :], ACT.Exp, bias=neg_max_all[:, t:t + 1],
                                                accum_out=comb_sum[:, t:t + 1])
                last.then_inc(cexp_ready, 1)

            def disp_exp(b):
                act.wait_ge(slotmax_ready, b + 1)
                wait(act, disp_done, b)
                for c in range(EC):
                    last = nc.scalar.activation(dispT[:, c, :], misc_b[:, c * N:(c + 1) * N], ACT.Exp,
                                                bias=neg_max_slot[:, c:c + 1], accum_out=disp_sum[:, c:c + 1])
                last.then_inc(dexp_ready, 1)

            def disp_high(b):
                act.wait_ge(disp_done, b + 1)
                wait(act, slotin_done, b)
                copy(disp_h[:, :, :].rearrange("p t e -> p (t e)"), misc_a[:, :]).then_inc(disph_ready, 1)

            def combT_high(b):
                act.wait_ge(combT_done, b + 1)
                copy(combT_h[:, bass.ds(b, 1), :, :].rearrange("p o c n -> p (o c n)"), misc_b[:, :]).then_inc(combTh_ready, 1)

            def slot_in_copy(b):
                act.wait_ge(slotin_done, b + 1)
                copy(slot_in[:, :, bass.ds(b, 1), :, :].rearrange("p c o e s -> p c (o e s)"),
                     misc_a[:, :].rearrange("p (c n) -> p c n", c=DC)).then_inc(slotin_ready, 1)

            nc.scalar.preload_act_table_set("natural_log_exp_and_others")
            guess1(0)

            def wq_high(c):
                n = slice(c * INNER // 2, (c + 1) * INNER // 2)
                act.wait_ge(wq_loaded[c], 16)
                copy(wq_h[:, :, n], wq_raw[:, :, n]).then_inc(wqh_ready, 1)

            wq_high(0)
            ctxT_copy(0)
            ctxT_move(0)
            xT_high(0)
            act.wait_ge(gates_loaded, 32)
            nc.scalar.activation(tanhs[:, :], gates[:, :], ACT.Tanh).then_inc(tanh_ready, 1)
            nc.scalar.preload_act_table_set("natural_log_exp_and_others")
            act.wait_ge(zeros_ready, 4)
            proj_high(0, 0)
            proj_high(0, 1)
            wq_high(1)
            proj_high(0, 2)
            exps(0, 0)

            def first_prep(p):
                if p == 4:
                    act.wait_ge(b1T_done, 1)
                    copy(b1T[:, :], misc_b[0:H, 0:E]).then_inc(b1T_ready, 1)
                if p < 4:
                    act.wait_ge(wo_loaded, 16)
                    c = slice(p * PAIRS // 4, (p + 1) * PAIRS // 4)
                    copy(wo_h[:, c, :], wo_raw[:, c, :]).then_inc(woh_ready, 1)
                if p == 4:
                    act.wait_ge(muss_ready, 1)
                    guess(mu_nt[:, 2, :], mu_nt[:, 1, :], mu_nt[:, 0, :], mu_act, 1, LN_SHIFT).then_inc(muguess_ready, 1)
                if p == 7:
                    act.wait_ge(muunit_ready, 1)
                    copy(mu_h[:, :, :], mu_sq[:, :, :]).then_inc(muh_ready, 1)

            def step_loop(b, first, last):
                for p in range(PAIRS):
                    if not first:
                        if p == 6:
                            comb_exp(b - 1)
                        if p == 7:
                            disp_high(b - 1)
                    near(exps, b, p, 1, first, last)
                    if not last:
                        if p == 0:
                            ctxT_copy(b + 1)
                        if p == 4:
                            xT_high(b + 1)
                    if not first:
                        if p == 5:
                            disp_exp(b - 1)
                        if p == 7:
                            combT_high(b - 1)
                    near(proj_high, b, p, AHEAD, first, last)
                    if not last and p == 0:
                        guess1(b + 1)
                    if not first:
                        if p == 3:
                            square_sums(b - 1)
                            xn2T_high(b - 1)
                        if p == 4:
                            logits_scaled(b - 1)
                    probT_high(b, p)
                    if not first:
                        if p == 2:
                            guess2(b - 1)
                        if p == 3:
                            xn2_high(b - 1)
                    near(attn_high, b, p, -1, first, last)
                    if not last and p == 4:
                        ctxT_move(b + 1)
                    if not first:
                        if p == 3:
                            guess3(b - 1)
                        if p == 7:
                            slot_in_copy(b - 1)
                    if first:
                        first_prep(p)

            batches(nc.scalar, step_loop)
            attn_high(B - 1, PAIRS - 1)
            guess2(B - 1)
            square_sums(B - 1)
            xn2T_high(B - 1)
            guess3(B - 1)
            xn2_high(B - 1)

            def gelus(k):
                act.wait_ge(hid_done, k + 1)
                for i in range(EQ):
                    e = k * EQ + i
                    last = nc.scalar.activation(hidT[0:H, e, :, :].rearrange("h s b -> h b s"),
                                                hid_ps[k][0:H, i * P:(i + 1) * P].rearrange("h (b s) -> h b s", s=S), ACT.Gelu,
                                                bias=b1T[:, e:e + 1])
                last.then_inc(hid_ready, 1)

            def so_high(b):
                act.wait_ge(so_back, b + 1)
                wait(act, mix_done, b - MR + 1)
                copy(so_h[:, b % MR, :, :].rearrange("p k d -> p (k d)"), back_ps[b % 2][:, :]).then_inc(soh_ready, 1)

            logits_scaled(B - 1)
            disp_exp(B - 1)
            comb_exp(B - 1)
            act.wait_ge(b1T_ready, 1)
            disp_high(B - 1)
            combT_high(B - 1)
            slot_in_copy(B - 1)
            for k in range(E // EQ):
                gelus(k)
            for b in range(B):
                so_high(b)

        @block.vector
        def _(dve):
            V = nc.vector

            def split(dst_l, src, dst_h, scale=None):
                if scale is None:
                    return V.tensor_tensor(dst_l, src, dst_h.bitcast(F32), ALU.subtract)
                return V.scalar_tensor_tensor(dst_l, src, scale, dst_h.bitcast(F32), ALU.mult, ALU.subtract)

            def link(ins, chain, n):
                ins.then_inc(chain, 1)
                dve.wait_ge(chain, n)

            def hold():
                V.memset(pause[:, :], 0.0)

            def newton(t, chain, n):
                link(V.scalar_tensor_tensor(t[:, 3, :], t[:, 2, :], -0.5, t[:, 2, :], ALU.mult, ALU.mult), chain, n)
                link(V.tensor_tensor(t[:, 3, :], t[:, 3, :], t[:, 0, :], ALU.mult), chain, n + 1)
                return V.scalar_tensor_tensor(t[:, 4, :], t[:, 3, :], 1.5, t[:, 2, :], ALU.add, ALU.mult)

            NORM1 = 2 + 3
            FFN = 3 + 3 + 4 + 2

            def moments(tile_of, stats, mv, chain, n):
                for t in range(NT):
                    last = V.bn_stats(stats[:, t, :], tile_of(t))
                link(last, chain, n)
                hold()
                for t in range(NT):
                    last = V.bn_aggr(mv[:, t, :], stats[:, t, :])
                link(last, chain, n + 1)

            def x_tile(b, t):
                return x_all[:, bass.ds(b, 1), t, :].rearrange("p o d -> p (o d)")

            def norm1_stats(b, loaded):
                dve.wait_ge(loaded, 16)
                moments(lambda t: x_tile(b, t), stats1, mv1, norm1_chain, NORM1 * b + 1)
                V.tensor_scalar(nt1[:, 0, :], mv1[:, :, 1], 1.0, LN_EPS, ALU.mult, ALU.add).then_inc(var1_ready, 1)

            def norm1(b):
                dve.wait_ge(guess1_ready, b + 1)
                link(newton(nt1, norm1_chain, NORM1 * b + 3), norm1_chain, NORM1 * b + 5)
                wait(dve, xT_done, b)
                for t in range(NT):
                    last = V.tensor_scalar(xn[:, t, :], x_tile(b, t), mv1[:, t, 0:1], nt1[:, 4, t:t + 1],
                                           ALU.subtract, ALU.mult)
                last.then_inc(xn_ready, 1)

            def xT_low(b):
                dve.wait_ge(xTh_ready, b + 1)
                split(xT_l[:, :, :].rearrange("p c n -> p (c n)"), misc_a[:, :],
                      xT_h[:, :, :].rearrange("p c n -> p (c n)")).then_inc(xTl_ready, 1)

            def proj_low(b, p):
                g, q, ps = 8 * b + p, p % QR, proj_ps[p % 2]
                dve.wait_ge(projh_ready, g + 1)
                split(q_l[:, q, :], ps[:, 0:N], q_h[:, q, :], QK_SCALE)
                for h in range(2):
                    c = slice(h * HEAD, (h + 1) * HEAD)
                    m = slice(h * M, (h + 1) * M)
                    split(k_l[c, q, m], ps[c, N:N + M], k_h[c, q, m])
                split(v_cols(v_l, p), ps[0:M, N + M:N + M + P].rearrange("m (h d) -> m h d", h=2),
                      v_cols(v_h, p)).then_inc(projl_ready, 1)

            def maxima(b, p):
                g, r = 8 * b + p, p % 2
                dve.wait_ge(scores_done, g + 1)
                wait(dve, exp_done, g - 1)
                V.tensor_reduce(neg_max[:, r, :], scores_ps[r][:, 0:4 * M].rearrange("p (j m) -> p j m", m=M),
                                axis=AX.X, op=ALU.max, negate=True).then_inc(negmax_ready, 1)

            def probT_low(b, p):
                g, r = 8 * b + p, p % 2
                dve.wait_ge(pth_ready, g + 1)
                split(probT_l[:, r, :], probT_ps[0:M, :], probT_h[:, r, :]).then_inc(ptl_ready, 1)

            def attn_low(b, p):
                g = 8 * b + p
                dve.wait_ge(attnh_ready, g + 1)
                split(attn_l[:, p, :], attn_ps[:, 0:N], attn_h[:, p, :]).then_inc(attnl_ready, 1)

            def reciprocals(b, p):
                g, r = 8 * b + p, p % 2
                dve.wait_ge(exp_done, g + 1)
                wait(dve, prob_ready, g - 1)
                V.reciprocal(prob_rec[:, r, :], prob_sum[:, r, :]).then_inc(rec_ready, 1)

            def x1_stats(b, y_ps=(misc_a, misc_b)):
                dve.wait_ge(y_done, b + 1)
                dve.wait_ge(xb_ready, b + 1)
                dve.wait_ge(tanh_ready, 1)
                for t in range(NT):
                    last = V.scalar_tensor_tensor(x_tile(b, t), y_ps[t][:, 0:D], tanhs[:, 0:1], x_tile(b, t),
                                                  ALU.mult, ALU.add)
                last.then_inc(x1_ready, 1)
                dve.wait_ge(x1_ready, b + 1)
                hold()
                moments(lambda t: x_tile(b, t), stats2, mv2, ffn_chain, FFN * b + 1)
                V.tensor_scalar(nt2[:, 0, :], mv2[:, :, 1], 1.0 + LN_EPS, LN_EPS * LN_EPS, ALU.mult, ALU.add)\
                    .then_inc(var2_ready, 1)

            def x1_gamma(b):
                dve.wait_ge(small_loaded, 16 * 5)
                wait(dve, xn2l_ready, b)
                wait(dve, xn2T_done, b)
                for t in range(NT):
                    last = V.scalar_tensor_tensor(xn2[:, t, :], x_tile(b, t), mv2[:, t, 0:1], gamma[:, :],
                                                  ALU.subtract, ALU.mult)
                link(last, ffn_chain, FFN * b + 3)

            def x1_hat(b):
                dve.wait_ge(guess2_ready, b + 1)
                link(newton(nt2, ffn_chain, FFN * b + 4), ffn_chain, FFN * b + 6)
                for t in range(NT):
                    last = V.scalar_tensor_tensor(xn2[:, t, :], xn2[:, t, :], nt2[:, 4, t:t + 1], beta[:, :],
                                                  ALU.mult, ALU.add)
                last.then_inc(xn2_ready, 1)

            def guard_norm(b):
                dve.wait_ge(ss_ready, b + 1)
                V.tensor_scalar_max(nt3[:, 0, :], nt3[:, 5, :], NORM_EPS * NORM_EPS).then_inc(ssm_ready, 1)

            def token_scale(b):
                dve.wait_ge(guess3_ready, b + 1)
                n = FFN * b + 7
                link(V.tensor_scalar_mul(nt3[:, 2, :], nt3[:, 2, :], float(2 ** (LN_SHIFT // 2))), ffn_chain, n)
                link(newton(nt3, ffn_chain, n + 1), ffn_chain, n + 3)
                wait(dve, logit_ready, b)
                V.tensor_scalar(nt3[:, 6, :], nt3[:, 4, :], scale_t[:, 0:1], None, ALU.mult).then_inc(rs_ready, 1)

            def xn2T_low(b):
                dve.wait_ge(xn2Th_ready, b + 1)
                split(xn2T_l[:, :, :].rearrange("p c n -> p (c n)"), misc_b[:, :],
                      xn2T_h[:, :, :].rearrange("p c n -> p (c n)")).then_inc(xn2Tl_ready, 1)

            def comb_max(b):
                dve.wait_ge(logit_ready, b + 1)
                V.tensor_reduce(neg_max_all[:, :], logit[:, :, :], axis=AX.X, op=ALU.max,
                                negate=True).then_inc(allmax_ready, 1)

            def disp_max(b):
                dve.wait_ge(logitT_done, b + 1)
                V.tensor_reduce(neg_max_slot[:, :], misc_b[:, :].rearrange("p (c n) -> p c n", c=EC), axis=AX.X, op=ALU.max,
                                negate=True).then_inc(slotmax_ready, 1)

            def comb_norm(b):
                dve.wait_ge(cexp_ready, b + 1)
                link(V.reciprocal(comb_rec[:, :], comb_sum[:, :]), ffn_chain, FFN * b + 12)
                for t in range(NT):
                    last = V.tensor_scalar(comb[:, t, :], comb[:, t, :], comb_rec[:, t:t + 1], None, ALU.mult)
                last.then_inc(comb_ready, 1)

            def disp_norm(b):
                dve.wait_ge(dexp_ready, b + 1)
                link(V.reciprocal(disp_rec[:, :], disp_sum[:, :]), ffn_chain, FFN * b + 11)
                for c in range(EC):
                    last = V.tensor_scalar(dispT[:, c, :], dispT[:, c, :], disp_rec[:, c:c + 1], None, ALU.mult)
                last.then_inc(dispT_ready, 1)

            def disp_low(b):
                dve.wait_ge(disph_ready, b + 1)
                split(disp_l[:, :, :].rearrange("p t e -> p (t e)"), misc_a[:, :],
                      disp_h[:, :, :].rearrange("p t e -> p (t e)")).then_inc(displ_ready, 1)

            def combT_low(b):
                dve.wait_ge(combTh_ready, b + 1)
                ct = [c[:, bass.ds(b, 1), :, :].rearrange("p o c n -> p (o c n)") for c in (combT_h, combT_l)]
                split(ct[1], misc_b[:, :], ct[0]).then_inc(combTl_ready, 1)

            for t in (k_h, k_l):
                V.memset(t[:, :, :].rearrange("p r m -> p (r m)").bitcast(F32), 0.0).then_inc(zeros_ready, 1)
            norm1_stats(0, x0_loaded)
            norm1(0)

            half = slice(0, INNER // 2)
            dve.wait_ge(wqh_ready, 1)
            split(wq_l[:, :, half], wq_raw[:, :, half], wq_h[:, :, half]).then_inc(wql_ready, 1)
            xT_low(0)
            for p in range(AHEAD):
                proj_low(0, p)
            for p in range(AHEAD_S):
                maxima(0, p)
            reciprocals(0, 0)

            def first_prep(p):
                if p == 1:
                    dve.wait_ge(small_loaded, 16 * 5)
                    dve.wait_ge(tanh_ready, 1)
                    V.tensor_scalar(bo_t[:, :], bo_t[:, :], tanhs[:, 0:1], None, ALU.mult).then_inc(bo_ready, 1)
                if p == 2:
                    dve.wait_ge(munorm_done, 1)
                    V.tensor_scalar_max(mu_nt[:, 0, :], misc_b[:, 0:ES], NORM_EPS * NORM_EPS).then_inc(muss_ready, 1)
                if p == 5:
                    dve.wait_ge(muguess_ready, 1)
                    link(V.tensor_scalar_mul(mu_nt[:, 2, :], mu_nt[:, 2, :], float(2 ** (LN_SHIFT // 2))), mu_chain, 1)
                    newton(mu_nt, mu_chain, 2).then_inc(murn_ready, 1)
                if p == 7:
                    dve.wait_ge(muh_ready, 1)
                    split(mu_l[:, :, :], mu_sq[:, :, :], mu_h[:, :, :]).then_inc(mul_ready, 1)

            def step_loop(b, first, last):
                for p in range(PAIRS):
                    if not last and p == 1:
                        norm1(b + 1)
                    if not first and p == 5:
                        comb_max(b - 1)
                    near(reciprocals, b, p, 1, first, last)
                    if not last:
                        if p == 0:
                            norm1_stats(b + 1, x_loaded)
                        if p == 4:
                            xT_low(b + 1)
                    if not first:
                        if p == 2:
                            x1_gamma(b - 1)
                        if p == 3:
                            guard_norm(b - 1)
                        if p == 5:
                            disp_norm(b - 1)
                    near(maxima, b, p, AHEAD_S, first, last)
                    near(proj_low, b, p, AHEAD, first, last)
                    if not first:
                        if p == 2:
                            x1_hat(b - 1)
                        if p == 3:
                            xn2T_low(b - 1)
                        if p == 7:
                            combT_low(b - 1)
                    probT_low(b, p)
                    if not first:
                        if p == 1:
                            x1_stats(b - 1)
                        if p == 3:
                            token_scale(b - 1)
                        if p == 4:
                            disp_max(b - 1)
                    near(attn_low, b, p, -1, first, last)
                    if not first:
                        if p == 5:
                            comb_norm(b - 1)
                        if p == 6:
                            disp_low(b - 1)
                    if first:
                        first_prep(p)

            batches(nc.vector, step_loop)
            attn_low(B - 1, PAIRS - 1)
            x1_stats(B - 1, y_last_ps)
            x1_gamma(B - 1)
            x1_hat(B - 1)
            guard_norm(B - 1)
            xn2T_low(B - 1)
            token_scale(B - 1)

            def so_copy(i):
                k, c = divmod(i, DC)
                dve.wait_ge(so_done, i + 1)
                V.tensor_copy(soT[:, c, k * EQ:(k + 1) * EQ, :, :].rearrange("p e s b -> p (e s b)"),
                              so_ps[i % 4][:, :]).then_inc(so_ready, 1)

            def so_low(b):
                dve.wait_ge(soh_ready, b + 1)
                split(so_l[:, b % MR, :, :].rearrange("p k d -> p (k d)"), back_ps[b % 2][:, :],
                      so_h[:, b % MR, :, :].rearrange("p k d -> p (k d)")).then_inc(sol_ready, 1)

            def mix_out(b):
                dve.wait_ge(mix_done, b + 1)
                if b >= MR:
                    dve.wait_ge(out_sent[b % MR], 16 * (b // MR))
                V.scalar_tensor_tensor(out_t[:, b % MR, :, :].rearrange("p t d -> p (t d)"), mix_ps[b % 2][:, :],
                                       tanhs[:, 1:2], x_all[:, b, :, :].rearrange("p t d -> p (t d)"),
                                       ALU.mult, ALU.add).then_inc(out_ready, 1)

            disp_max(B - 1)
            comb_max(B - 1)
            disp_norm(B - 1)
            comb_norm(B - 1)
            disp_low(B - 1)
            combT_low(B - 1)
            for i in range(E // EQ * DC):
                so_copy(i)
            so_low(0)
            for b in range(B):
                if b + 1 < B:
                    so_low(b + 1)
                mix_out(b)

        @block.tensor
        def _(pe):
            def product(o, terms, start=True, stop=True):
                n = 3 * len(terms)
                i = 0
                for ah, al, bh, bl in terms:
                    for lhs, rhs in ((ah, bh), (ah, bl), (al, bh)):
                        last = nc.tensor.matmul(o, lhs, rhs, start=start and i == 0, stop=stop and i == n - 1)
                        i += 1
                return last

            def xT(b):
                pe.wait_ge(xn_ready, b + 1)
                pe.wait_ge(ctxT_staged, b + 1)
                wait(pe, x1_ready, b - 1)
                for t in range(NT):
                    for c in range(DC):
                        last = nc.tensor.transpose(misc_a[:, c * N + t * P:c * N + (t + 1) * P],
                                                   xn[:, t, c * P:(c + 1) * P], ident[:, :])
                last.then_inc(xT_done, 1)

            def transpose_ctx(b):
                pe.wait_ge(ctx_loaded, 16 * (b + 1))
                wait(pe, xTl_ready, b)
                wait(pe, slotin_ready, b - 2)
                nc.tensor.transpose(misc_a[:, 0:M], ctx_in[:, :], ident[0:M, 0:M]).then_inc(ctxT_done, 1)

            def project(b, p):
                g, ps = 8 * b + p, proj_ps[p % 2]
                if p == 0:
                    pe.wait_ge(xTl_ready, b + 1)
                    pe.wait_ge(ctxT_ready, b + 1)
                wait(pe, projl_ready, g - 1)
                c = slice(p * P, (p + 1) * P)
                product(ps[:, 0:N], [(wq_h[:, k, c], wq_l[:, k, c], xT_h[:, k, :], xT_l[:, k, :]) for k in range(DC)])
                if isinstance(g, int) and g == 0:
                    pe.wait_ge(wkv_loaded, 32)
                nc.tensor.matmul(ps[:, N:N + M], wk[:, c], ctxT[:, :], start=True, stop=True)
                nc.tensor.matmul(ps[0:M, N + M:N + M + P], ctxT[:, :], wv[:, c], start=True, stop=True)\
                    .then_inc(proj_done, 1)

            def score(b, p):
                g, r, q = 8 * b + p, p % 2, p % QR
                pe.wait_ge(projl_ready, g + 1)
                wait(pe, exp_done, g - 1)
                for t in range(NT):
                    c = slice(t * P, (t + 1) * P)
                    last = product(scores_ps[r][:, t * K2:(t + 1) * K2],
                                   [(q_h[:, q, c], q_l[:, q, c], k_h[:, q, :], k_l[:, q, :])])
                last.then_inc(scores_done, 1)

            def transpose_prob(b, p):
                g, r = 8 * b + p, p % 2
                pe.wait_ge(prob_ready, g + 1)
                wait(pe, ptl_ready, g)
                for h in range(2):
                    for t in range(NT):
                        o = h * N + t * P
                        last = nc.tensor.transpose(probT_ps[0:M, o:o + P], prob[:, r, t, h, :], ident[:, :])
                last.then_inc(probT_done, 1)

            def attend(b, p):
                g, r, v = 8 * b + p, p % 2, p % VR
                pe.wait_ge(ptl_ready, g + 1)
                wait(pe, attnl_ready, g)
                product(attn_ps[:, 0:N], [(v_h[:, v, h, :], v_l[:, v, h, :], probT_h[:, r, h * N:(h + 1) * N],
                                           probT_l[:, r, h * N:(h + 1) * N]) for h in range(2)]).then_inc(attn_done, 1)

            def output_projection(b, begin, end, context_between=True, y_ps=(misc_a, misc_b)):
                if begin == 0:
                    pe.wait_ge(wol_ready, 4)
                    if y_ps is y_last_ps:
                        pe.wait_ge(projl_ready, 8 * B)
                    else:
                        wait(pe, combTl_ready, b)
                        if context_between:
                            pe.wait_ge(ctxT_staged, b + 3)
                        else:
                            wait(pe, slotin_ready, b)
                pe.wait_ge(attnl_ready, 8 * b + end)
                for t in range(NT):
                    c = slice(t * P, (t + 1) * P)
                    last = product(y_ps[t][:, 0:D],
                                   [(attn_h[:, k, c], attn_l[:, k, c], wo_h[:, k, :], wo_l[:, k, :])
                                    for k in range(begin, end)],
                                   start=begin == 0, stop=end == PAIRS)
                if end == PAIRS:
                    last.then_inc(y_done, 1)

            def transpose_xn2(b):
                pe.wait_ge(xn2_ready, b + 1)
                for t in range(NT):
                    for c in range(DC):
                        last = nc.tensor.transpose(misc_b[:, c * N + t * P:c * N + (t + 1) * P],
                                                   xn2[:, t, c * P:(c + 1) * P], ident[:, :])
                last.then_inc(xn2T_done, 1)

            def logits(b):
                pe.wait_ge(xn2Tl_ready, b + 1)
                pe.wait_ge(mul_ready, 1)
                for t in range(NT):
                    c = slice(t * P, (t + 1) * P)
                    last = product(misc_b[:, t * ES:(t + 1) * ES],
                                   [(xn2T_h[:, k, c], xn2T_l[:, k, c], mu_h[:, k, :], mu_l[:, k, :]) for k in range(DC)])
                last.then_inc(logits_done, 1)

            def transpose_logits(b):
                pe.wait_ge(logit_ready, b + 1)
                for c in range(EC):
                    for t in range(NT):
                        last = nc.tensor.transpose(misc_b[:, c * N + t * P:c * N + (t + 1) * P],
                                                   logit[:, t, c * P:(c + 1) * P], ident[:, :])
                last.then_inc(logitT_done, 1)

            def transpose_disp(b):
                pe.wait_ge(dispT_ready, b + 1)
                for t in range(NT):
                    for c in range(EC):
                        last = nc.tensor.transpose(misc_a[:, t * ES + c * P:t * ES + (c + 1) * P],
                                                   dispT[:, c, t * P:(t + 1) * P], ident[:, :])
                last.then_inc(disp_done, 1)

            def transpose_comb(b):
                pe.wait_ge(comb_ready, b + 1)
                for c in range(EC):
                    for t in range(NT):
                        last = nc.tensor.transpose(misc_b[:, c * N + t * P:c * N + (t + 1) * P],
                                                   comb[:, t, c * P:(c + 1) * P], ident[:, :])
                last.then_inc(combT_done, 1)

            def slot_inputs(b):
                pe.wait_ge(displ_ready, b + 1)
                pe.wait_ge(xn2l_ready, b + 1)
                for c in range(DC):
                    d = slice(c * P, (c + 1) * P)
                    last = product(misc_a[:, c * ES:(c + 1) * ES],
                                   [(xn2_h[:, t, d], xn2_l[:, t, d], disp_h[:, t, :], disp_l[:, t, :]) for t in range(NT)])
                last.then_inc(slotin_done, 1)

            pe.wait_ge(ident_ready, 1)
            transpose_ctx(0)
            xT(0)
            pe.wait_ge(wql_ready, 1)
            for p in range(AHEAD):
                project(0, p)
            for p in range(AHEAD_S):
                score(0, p)

            def step_loop(b, first, last):
                for p in range(PAIRS):
                    if first and p == PAIRS // 2 - AHEAD:
                        pe.wait_ge(wql_half_ready, 1)
                    if not first and p == 7:
                        transpose_comb(b - 1)
                    near(project, b, p, AHEAD, first, last)
                    if not first and p == 1:
                        output_projection(b - 1, 0, PAIRS // 2, not last)
                    near(score, b, p, AHEAD_S, first, last)
                    if not last and p == 0:
                        transpose_ctx(b + 1)
                    if not last and p == 3:
                        xT(b + 1)
                    if not first and p == 3:
                        transpose_xn2(b - 1)
                    if not first and p == 4:
                        logits(b - 1)
                    if last and p == 6:
                        output_projection(b, 0, PAIRS // 2, y_ps=y_last_ps)
                    transpose_prob(b, p)
                    if not first and p == 1:
                        output_projection(b - 1, PAIRS // 2, PAIRS)
                    near(attend, b, p, -1, first, last)
                    if not first and p == 4:
                        transpose_logits(b - 1)
                    if not first and p == 5:
                        transpose_disp(b - 1)
                    if not first and p == 7:
                        slot_inputs(b - 1)
                    if first and p == 1:
                        pe.wait_ge(musq_ready, 1)
                        for c in range(DC):
                            mm = nc.tensor.matmul(misc_b[:, 0:ES], ones[:, :], mu_sq[:, c, :],
                                                  start=c == 0, stop=c == DC - 1)
                        mm.then_inc(munorm_done, 1)
                    if first and p == 3:
                        pe.wait_ge(muss_ready, 1)
                        pe.wait_ge(small_loaded, 16 * 5)
                        nc.tensor.transpose(misc_b[0:H, 0:E], b1_in[:, :], ident[0:E, 0:E]).then_inc(b1T_done, 1)
                    if first and p == 7:
                        pe.wait_ge(b1T_ready, 1)

            batches(nc.tensor, step_loop)
            attend(B - 1, PAIRS - 1)
            output_projection(B - 1, PAIRS // 2, PAIRS - 2, y_ps=y_last_ps)
            output_projection(B - 1, PAIRS - 2, PAIRS, y_ps=y_last_ps)

            def hidden(k):
                for i in range(EQ):
                    e = k * EQ + i
                    for c in range(DC):
                        last = nc.tensor.matmul(hid_ps[k][0:H, i * P:(i + 1) * P], w1_t[:, e, c, :],
                                                slot_in[:, c, :, e, :], start=c == 0, stop=c == DC - 1)
                last.then_inc(hid_done, 1)

            def outputs(k):
                for c in range(DC):
                    i = k * DC + c
                    wait(pe, so_ready, i - 3)
                    for j in range(EQ):
                        e = k * EQ + j
                        last = nc.tensor.matmul(so_ps[i % 4][:, j * P:(j + 1) * P], w2_t[:, e, c * P:(c + 1) * P],
                                                hidT[:, e, :, :].rearrange("h s b -> h (s b)"), start=True, stop=True)
                    last.then_inc(so_done, 1)

            def transpose_back(b):
                pe.wait_ge(so_ready, E // EQ * DC)
                wait(pe, sol_ready, b - 1)
                for k in range(EC):
                    for c in range(DC):
                        last = nc.tensor.transpose(back_ps[b % 2][:, k * D + c * P:k * D + (c + 1) * P],
                                                   soT[:, c, k * E // EC:(k + 1) * E // EC, :, b].rearrange("p e s -> p (e s)"),
                                                   ident[:, :])
                last.then_inc(so_back, 1)

            def combine(b):
                pe.wait_ge(sol_ready, b + 1)
                wait(pe, out_ready, b - 1)
                for t in range(NT):
                    c = slice(t * P, (t + 1) * P)
                    last = product(mix_ps[b % 2][:, t * D:(t + 1) * D],
                                   [(combT_h[:, b, k, c], combT_l[:, b, k, c], so_h[:, b % MR, k, :], so_l[:, b % MR, k, :])
                                    for k in range(EC)])
                last.then_inc(mix_done, 1)

            transpose_xn2(B - 1)
            logits(B - 1)
            transpose_logits(B - 1)
            transpose_disp(B - 1)
            transpose_comb(B - 1)
            slot_inputs(B - 1)
            pe.wait_ge(exp_loaded, 48)
            pe.wait_ge(attnl_ready, B * PAIRS)
            pe.wait_ge(slotin_ready, B)
            for k in range(E // EQ):
                hidden(k)
            pe.wait_ge(ones_ready, 1)
            for k in range(E // EQ):
                pe.wait_ge(hid_ready, k + 1)
                outputs(k)
            transpose_back(0)
            for b in range(1, B):
                transpose_back(b)
                combine(b - 1)
            combine(B - 1)


_INS = ['x', 'ctx_512', 'g_xattn', 'g_ffn', 'L0_xattn_Wq', 'L0_xattn_Wk', 'L0_xattn_Wv', 'L0_xattn_Wo', 'L0_xattn_bo',
        'L0_ffn_ln_gamma', 'L0_ffn_ln_beta', 'L0_ffn_mu', 'L0_ffn_scale', 'L0_ffn_w1', 'L0_ffn_b1', 'L0_ffn_w2', 'L0_ffn_b2']


def kernel(**inputs):
    import concourse.bacc as _bacc
    from concourse.bass_utils import run_bass_kernel_spmd as _run

    nc = _bacc.Bacc("TRN2", target_bir_lowering=False, num_devices=1)
    arrays, args = {}, []
    for name in _INS:
        a = np.ascontiguousarray(inputs[name])
        arrays[f"in_{name}_dram"] = a
        args.append(nc.dram_tensor(f"in_{name}_dram", a.shape, mybir.dt.from_np(a.dtype), kind="ExternalInput").ap())
    shape = inputs['x'].shape
    args.append(nc.dram_tensor("out_0_dram", shape, F32, kind="ExternalOutput").ap())
    flamingo_layer(nc, *args)
    r = _run(nc, [arrays], core_ids=[0])
    return r.results[0]["out_0_dram"]
```
